# Optimizing a Trainium2 kernel written in Bass

```python
import numpy as np
import jax
import jax.numpy as jnp

def _softmax(x, axis=-1):
    return jax.nn.softmax(x, axis=axis)

def _gelu(x):
    return jax.nn.gelu(x, approximate=True)

def _silu(x):
    return jax.nn.silu(x)

def _sigmoid(x):
    return jax.nn.sigmoid(x)

def _layernorm(x, axis=-1, eps=1e-05):
    m = jnp.mean(x, axis=axis, keepdims=True)
    v = jnp.var(x, axis=axis, keepdims=True)
    return (x - m) / jnp.sqrt(v + eps)

def _scatter_add(tgt, idx, src, axis=0):
    return tgt.at[idx].add(src)

def _segment_sum(src, seg, n):
    return jax.ops.segment_sum(src, seg, n)
kernel_name = 'mk_flamingo_gated_d1_seqx_r8_8a0301'

def setup_inputs(seed: int=0):
    np.random.seed(seed)
    _w = jnp.asarray

    def _rec_inputs():
        import jax
        import jax.numpy as jnp
        _rk = jax.random.key(seed)
        x = -0.0002928 + 1 * jax.random.normal(jax.random.fold_in(_rk, 1), (128, 64, 128), jnp.float32)
        _lenS = 64 - jax.random.randint(jax.random.fold_in(_rk, 7), (128,), 0, max(1, 64 // 4) + 1, jnp.int32)
        _lenS2 = 64 - jax.random.randint(jax.random.fold_in(_rk, 8), (128,), 0, max(1, 64 // 4) + 1, jnp.int32)
        _ctx_1024P = jax.random.normal(jax.random.fold_in(_rk, 11), (128, 16, 128), jnp.float32)
        _ctx_1024c = jax.random.dirichlet(jax.random.fold_in(_rk, 511), 0.3 * jnp.ones((16,), jnp.float32), (128, 64))
        _ctx_1024t = jnp.einsum('bsk,bkd->bsd', _ctx_1024c, _ctx_1024P)
        _ctx_1024t = _ctx_1024t * jax.lax.rsqrt(jnp.mean(jnp.square(_ctx_1024t)) + 1e-12) * 0.953939
        ctx_1024 = -1.39393e-06 + 0.999914 * (_ctx_1024t + 0.3 * jax.random.normal(jax.random.fold_in(_rk, 611), (128, 64, 128), jnp.float32))
        _g = jax.random.normal(jax.random.fold_in(_rk, 9001), (2, 1), jnp.float32)
        _g = jnp.sign(_g) * jnp.maximum(jnp.abs(_g), 1.0) + (_g == 0) * 1.0
        g_xattn = _g[0]
        g_ffn = _g[1]
        return (x, ctx_1024, g_xattn, g_ffn)
    x, ctx_1024, g_xattn, g_ffn = _rec_inputs()

    def _L0_xattn_setup():
        import jax, jax.numpy as jnp
        import numpy as np
        D_MODEL = 128
        NUM_HEADS = 16
        D_K = D_MODEL // NUM_HEADS

        def _split_heads(x):
            B, S, _ = x.shape
            return x.reshape(B, S, NUM_HEADS, D_K).transpose(0, 2, 1, 3)
        key = jax.random.key(seed)
        ks = jax.random.split(key, 11)
        B, S = (2, 256)
        scale = 1.0 / np.sqrt(D_MODEL)
        inp = {'q': jax.random.normal(ks[0], (B, S, D_MODEL), jnp.float32), 'k': jax.random.normal(ks[1], (B, S, D_MODEL), jnp.float32), 'v': jax.random.normal(ks[2], (B, S, D_MODEL), jnp.float32), 'W_q': jax.random.normal(ks[3], (D_MODEL, D_MODEL), jnp.float32) * scale, 'b_q': jnp.zeros((D_MODEL,), jnp.float32), 'W_k': jax.random.normal(ks[4], (D_MODEL, D_MODEL), jnp.float32) * scale, 'b_k': jnp.zeros((D_MODEL,), jnp.float32), 'W_v': jax.random.normal(ks[5], (D_MODEL, D_MODEL), jnp.float32) * scale, 'b_v': jnp.zeros((D_MODEL,), jnp.float32), 'W_o': jax.random.normal(ks[6], (D_MODEL, D_MODEL), jnp.float32) * scale, 'b_o': jnp.zeros((D_MODEL,), jnp.float32)}
        return inp
    _L0_xattn_all = _L0_xattn_setup()
    _L0_xattn_in = {k: v for k, v in _L0_xattn_all.items() if k in ('W_q', 'b_q', 'W_k', 'b_k', 'W_v', 'b_v', 'W_o', 'b_o')}
    del _L0_xattn_all

    def _L0_ffn_setup():
        import jax, jax.numpy as jnp
        import numpy as np
        B, T, E, C, H, G = (2, 256, 8, 128, 256, 16)
        key = jax.random.key(seed)
        ks = jax.random.split(key, 7)
        return {'hidden_states': jax.random.normal(ks[0], (B, T, C), jnp.float32), 'w_red': jax.random.normal(ks[1], (C, G), jnp.float32) * 0.02, 'wg': jax.random.normal(ks[2], (E, G), jnp.float32), 'W1': jax.random.normal(ks[3], (E, C, H), jnp.float32) * 0.02, 'b1': jax.random.normal(ks[4], (E, H), jnp.float32) * 0.02, 'W2': jax.random.normal(ks[5], (E, H, C), jnp.float32) * 0.02, 'b2': jax.random.normal(ks[6], (E, C), jnp.float32) * 0.02}
    _L0_ffn_all = _L0_ffn_setup()
    _L0_ffn_in = {k: v for k, v in _L0_ffn_all.items() if k in ('w_red', 'wg', 'W1', 'b1', 'W2', 'b2')}
    del _L0_ffn_all
    return {'x': x, 'ctx_1024': ctx_1024, 'g_xattn': g_xattn, 'g_ffn': g_ffn, 'L0_xattn_W_q': _L0_xattn_in['W_q'], 'L0_xattn_b_q': _L0_xattn_in['b_q'], 'L0_xattn_W_k': _L0_xattn_in['W_k'], 'L0_xattn_b_k': _L0_xattn_in['b_k'], 'L0_xattn_W_v': _L0_xattn_in['W_v'], 'L0_xattn_b_v': _L0_xattn_in['b_v'], 'L0_xattn_W_o': _L0_xattn_in['W_o'], 'L0_xattn_b_o': _L0_xattn_in['b_o'], 'L0_ffn_w_red': _L0_ffn_in['w_red'], 'L0_ffn_wg': _L0_ffn_in['wg'], 'L0_ffn_W1': _L0_ffn_in['W1'], 'L0_ffn_b1': _L0_ffn_in['b1'], 'L0_ffn_W2': _L0_ffn_in['W2'], 'L0_ffn_b2': _L0_ffn_in['b2']}

def reference(x, ctx_1024, g_xattn, g_ffn, L0_xattn_W_q, L0_xattn_b_q, L0_xattn_W_k, L0_xattn_b_k, L0_xattn_W_v, L0_xattn_b_v, L0_xattn_W_o, L0_xattn_b_o, L0_ffn_w_red, L0_ffn_wg, L0_ffn_W1, L0_ffn_b1, L0_ffn_W2, L0_ffn_b2):
    import jax
    import jax.numpy as jnp

    def _L0_xattn_ref(q, k, v, W_q, b_q, W_k, b_k, W_v, b_v, W_o, b_o):
        import jax, jax.numpy as jnp
        import numpy as np
        D_MODEL = 128
        NUM_HEADS = 16
        D_K = D_MODEL // NUM_HEADS

        def _split_heads(x):
            B, S, _ = x.shape
            return x.reshape(B, S, NUM_HEADS, D_K).transpose(0, 2, 1, 3)
        qh = _split_heads(q @ W_q + b_q)
        kh = _split_heads(k @ W_k + b_k)
        vh = _split_heads(v @ W_v + b_v)
        scores = jnp.einsum('bhqd,bhkd->bhqk', qh, kh) / jnp.sqrt(jnp.asarray(D_K, qh.dtype))
        probs = jax.nn.softmax(scores, axis=-1)
        ctx = jnp.einsum('bhqk,bhkd->bhqd', probs, vh)
        B, H, S, Dk = ctx.shape
        out = ctx.transpose(0, 2, 1, 3).reshape(B, S, D_MODEL)
        return out @ W_o + b_o

    def _L0_ffn_ref(hidden_states, w_red, wg, W1, b1, W2, b2):
        import jax, jax.numpy as jnp
        import numpy as np
        B, T, E, C, H, G = (2, 256, 8, 128, 256, 16)
        b, t, c = hidden_states.shape
        x = hidden_states.reshape(-1, c)
        x_red = x @ w_red
        wg_n = wg / jnp.maximum(jnp.linalg.norm(wg, axis=1, keepdims=True), 0.0001)
        logits = x_red @ wg_n.T
        gates = jax.nn.softmax(logits, axis=1)
        scores = jnp.max(gates, axis=1)
        idx = jnp.argmax(gates, axis=1)
        h = jnp.einsum('nc,ech->neh', x, W1) + b1[None]
        h = jnp.take_along_axis(h, idx[:, None, None], axis=1)[:, 0, :]
        h = jax.nn.gelu(h, approximate=False)
        o = jnp.einsum('nh,ehc->nec', h, W2) + b2[None]
        o = jnp.take_along_axis(o, idx[:, None, None], axis=1)[:, 0, :]
        o = o * scores[:, None]
        return o.reshape(b, t, c)
    x = x + jnp.tanh(g_xattn[0]) * _L0_xattn_ref(_layernorm(x, axis=-1), ctx_1024, ctx_1024, L0_xattn_W_q, L0_xattn_b_q, L0_xattn_W_k, L0_xattn_b_k, L0_xattn_W_v, L0_xattn_b_v, L0_xattn_W_o, L0_xattn_b_o)
    x = x + jnp.tanh(g_ffn[0]) * _L0_ffn_ref(_layernorm(x, axis=-1), L0_ffn_w_red, L0_ffn_wg, L0_ffn_W1, L0_ffn_b1, L0_ffn_W2, L0_ffn_b2)
    return x

_drawn_inputs = setup_inputs


def setup_inputs(seed=0):
    import zlib

    import numpy as np

    out = dict(_drawn_inputs(seed))
    spreads = {'L0_xattn_b_q': (0.0, 0.447),
     'L0_xattn_b_k': (0.0, 0.8),
     'L0_xattn_b_v': (0.0, 0.1),
     'L0_xattn_b_o': (0.0, 0.1)}
    factors = {'L0_ffn_w_red': 8.0,
     'L0_ffn_wg': 8.0,
     'L0_ffn_W1': 8.0,
     'L0_ffn_b1': 8.0,
     'L0_ffn_W2': 8.0,
     'L0_ffn_b2': 8.0}
    for name, (base, spread) in spreads.items():
        noise = np.random.default_rng([zlib.crc32(name.encode()), seed]).standard_normal(out[name].shape)
        drawn = base * np.exp(spread * noise) if base else spread * noise
        out[name] = jnp.asarray(drawn.astype(out[name].dtype))
    for name, factor in factors.items():
        out[name] = (out[name] * factor).astype(out[name].dtype)
    return out
```

```python
from contextlib import ExitStack

import concourse.bass as bass
from concourse import mybir

ALU = mybir.AluOpType
ACT = mybir.ActivationFunctionType
F32 = mybir.dt.float32
BF16 = mybir.dt.bfloat16
U32 = mybir.dt.uint32
I32 = mybir.dt.int32
AX_X = mybir.AxisListType.X

P = 128
D = 128
H = 16
DK = D // H
S = 64
B = 128
N = B * S
UNIT = P
CU = 4
CT = CU * UNIT
NC_ = N // CT
NU = N // UNIT
GH = 8
G = H // GH
HR = P // GH
CJ = 4
EPS = 1e-5
ISC = float(DK) ** -0.5
NE = 8
GD = 16
HID = 256
HH = HID // P
NT = N // P + NE
RW = D + 4
R_RSTD, R_MEAN, R_GATE, R_ID = D, D + 1, D + 2, D + 3
NB = 4


def gated_block(nc, x, ctx_in, g_xattn, g_ffn, W_q, b_q, W_k, b_k, W_v, b_v, W_o, b_o, w_red, wg, W1, b1, W2, b2, out):
    es = ExitStack()
    with es:
        def sb(name, shape, dt=F32):
            return es.enter_context(nc.sbuf_tensor(name, shape, dt))

        def pb(name, shape, dt=F32):
            return es.enter_context(nc.psum_tensor(name, shape, dt))

        def sem(name):
            return es.enter_context(nc.semaphore(name))

        x_t = x.rearrange("(t two) s d -> (two s) t d", two=2)
        c_t = ctx_in.rearrange("(t two) s d -> (two s) t d", two=2)
        out_rows = out.rearrange("b s d -> (b s) d")
        records = nc.dram_tensor("records", [NT * P, RW], F32, kind="Internal").ap()

        ident = sb("ident", [P, P])
        wq = sb("wq", [P, D])
        wk = sb("wk", [P, D])
        wk16 = sb("wk16", [P, G, GH, HR])
        wv = sb("wv", [P, D])
        wo = sb("wo", [P, 2, CJ, D])
        bq = sb("bq", [P, 1])
        bqs = sb("bqs", [P, 1])
        bkrow = sb("bkrow", [1, G, GH, HR])
        bk16 = sb("bk16", [P, G])
        one = sb("one", [1, 1])
        bv = sb("bv", [P, D])
        bo = sb("bo", [P, D])
        tgbo = sb("tgbo", [P, D])
        gx = sb("gx", [P, 1])
        tg = sb("tg", [P, 1])
        ksum = sb("ksum", [P, 32])
        mhalf = sb("mhalf", [P, CU])
        tri = sb("tri", [P, P], BF16)
        ones = sb("ones", [P, P], BF16)
        rank = sb("rank", [P, NE])
        tile_no = sb("tile_no", [P, NT])
        tile_i = sb("tile_i", [P, NT], I32)
        token = sb("token", [P, NU], I32)
        blank = sb("blank", [P, RW])
        tgf = sb("tgf", [P, 1])
        gf = sb("gf", [P, 1])
        wred = sb("wred", [P, GD])
        wredT = sb("wredT", [GD, P])
        wgs = sb("wgs", [NE, GD])
        wg2 = sb("wg2", [NE, GD])
        wgn = sb("wgn", [NE, GD])
        wgT = sb("wgT", [GD, NE])
        nrm = sb("nrm", [NE, 4])
        wc = sb("wc", [P, NE])
        b1s = sb("b1s", [NE * HH, P])
        b1c = sb("b1c", [P, NE, HH])
        eid = sb("eid", [P, NT], I32)
        pos = sb("pos", [P, NU], U32)
        oh = sb("oh", [P, NU, NE], BF16)
        XR = sb("XR", [P, NU, RW])
        X = XR[:, :, 0:D]
        XC = [sb(f"XC{i}", [P, CU, D]) for i in range(2)]
        C = [sb(f"C{i}", [P, CU, D]) for i in range(2)]
        st = sb("st", [P, CU, 6])
        mv = sb("mv", [P, CU, 2])
        ve = sb("ve", [P, CU])
        rstd = sb("rstd", [P, CU])
        shift = sb("shift", [P, CU])
        xn = sb("xn", [P, CU, D])
        xT = sb("xT", [P, CT])
        cT = sb("cT", [P, CT])
        qT = [sb(f"qT{i}", [P, CT]) for i in range(2)]
        qb = sb("qb", [P, CT], BF16)
        kT = [sb(f"kT{i}", [P, G, CT]) for i in range(2)]
        kb = sb("kb", [P, G, CT], BF16)
        Kd = [sb(f"Kd{i}", [P, H, CT], BF16) for i in range(2)]
        Qd = [sb(f"Qd{i}", [P, G, GH, CT]) for i in range(2)]
        V = [sb(f"V{i}", [P, CU, H, 32]) for i in range(2)]
        mx = sb("mx", [P, CU, H])
        mT = [sb(f"mT{i}", [H, CT]) for i in range(2)]
        PT = [sb(f"PT{i}", [P, H, S]) for i in range(2)]
        rec = sb("rec", [P, CJ * S])
        OT = [sb(f"OT{i}", [P, CJ, S]) for i in range(2)]

        lg, ex, ky, ta = (V[0][:, i].rearrange("p h r -> p (h r)").rearrange("p (u e) -> p u e", e=NE) for i in range(CU))
        tb, pf, tot, cmpb = (V[1][:, i].rearrange("p h r -> p (h r)").rearrange("p (u e) -> p u e", e=NE) for i in range(CU))
        small = PT[0][:, :, :].rearrange("p h q -> p (h q)")
        gT = [xT, cT]
        kd0 = Kd[0][:, :, :].rearrange("p h t -> p (h t)").bitcast(F32)
        kd1 = Kd[1][:, :, :].rearrange("p h t -> p (h t)").bitcast(F32)
        w1 = kd0[:, 0:NE * HID].rearrange("p (e h) -> p e h", e=NE)
        w2 = kd0[:, NE * HID:2 * NE * HID].rearrange("p (e m c) -> p e m c", e=NE, m=HH)
        b2r = kd1[:, 0:NE * D].rearrange("p (e c) -> p e c", e=NE)
        rr = [Qd[0][:, 0, i, 0:RW] for i in range(NB)]
        fo = [Qd[0][:, 1, i, 0:D] for i in range(NB)]
        ft = [Qd[0][:, 0, NB + i, 0:D] for i in range(2)]
        fx = [Qd[0][:, 0, NB + i, D:2 * D] for i in range(2)]
        fxT = [Qd[0][:, 0, NB + i, 2 * D:3 * D] for i in range(2)]
        w1s = [Qd[0][:, 1, NB + i, 0:HID] for i in range(2)]
        fh = [Qd[0][:, 1, NB + i, HID:2 * HID].rearrange("p (m t) -> p m t", m=HH) for i in range(2)]
        cmpt = Qd[1][:, 0, 0:2, :].rearrange("p a b -> p (a b)")[:, 0:NT * NE].rearrange("p (t e) -> p t e", e=NE)

        s2p = [pb(f"s2p{i}", [P, 512]) for i in range(2)]
        s1p = [pb(f"s1p{i}", [P, 512]) for i in range(2)]
        pvp = pb("pvp", [P, 512])
        m0 = pb("m0", [P, 512])
        m1 = pb("m1", [P, 512])
        m2 = pb("m2", [P, 512])

        w_in = sem("w_in")
        memset_done = sem("memset_done")
        x_in = [sem(f"x_in{i}") for i in range(2)]
        c_in = [sem(f"c_in{i}") for i in range(2)]
        kd_in = [sem(f"kd_in{i}") for i in range(2)]
        qd_in = [sem(f"qd_in{i}") for i in range(2)]
        setup_v = sem("setup_v")
        setup_a = sem("setup_a")
        setup_p = sem("setup_p")
        setup_t = sem("setup_t")
        stats = sem("stats")
        stat_step = sem("stat_step")
        rstd_ok = sem("rstd_ok")
        pool_step = sem("pool_step")
        xn_ok = sem("xn_ok")
        xb_ok = sem("xb_ok")
        xT_ps = sem("xT_ps")
        cT_ps = sem("cT_ps")
        xT_sb = sem("xT_sb")
        cT_sb = sem("cT_sb")
        q_ps = sem("q_ps")
        k_ps = sem("k_ps")
        v_ps = sem("v_ps")
        q_sb = sem("q_sb")
        k_sb = sem("k_sb")
        qb_ok = sem("qb_ok")
        kb_ok = sem("kb_ok")
        v_sb = sem("v_sb")
        s1_ps = sem("s1_ps")
        mx_ok = sem("mx_ok")
        mT_ps = sem("mT_ps")
        mT_sb = sem("mT_sb")
        s2_ps = sem("s2_ps")
        pt_ok = sem("pt_ok")
        pv_ps = sem("pv_ps")
        rec_ok = sem("rec_ok")
        ot_ok = sem("ot_ok")
        o_ps = sem("o_ps")
        x1_ok = sem("x1_ok")
        fill_ok = sem("fill_ok")
        passed = sem("passed")
        we_in = sem("we_in")
        nrm_ok = sem("nrm_ok")
        wgn_ok = sem("wgn_ok")
        wgT_ok = sem("wgT_ok")
        wc_ok = sem("wc_ok")
        chain = sem("chain")
        pchain = sem("pchain")
        gs1 = sem("gs1")
        g_stat = sem("g_stat")
        g_rstd = sem("g_rstd")
        g_xn = sem("g_xn")
        g_pay = sem("g_pay")
        g_tr = sem("g_tr")
        g_xT = sem("g_xT")
        g_lg = sem("g_lg")
        g_lgv = sem("g_lgv")
        diff_ok = sem("diff_ok")
        ex_ok = sem("ex_ok")
        oh_ok = sem("oh_ok")
        cnt_ps = sem("cnt_ps")
        pos_ok = sem("pos_ok")
        eid_ok = sem("eid_ok")
        gate_ok = sem("gate_ok")
        rec_out = sem("rec_out")
        r_in = [sem(f"r_in{i}") for i in range(NB)]
        f_xn = sem("f_xn")
        f_tr = sem("f_tr")
        f_xT = sem("f_xT")
        f_w = sem("f_w")
        f_h = sem("f_h")
        f_g = sem("f_g")
        f_o = sem("f_o")
        f_t = sem("f_t")
        f_out = sem("f_out")
        scat = [sem(f"scat{i}") for i in range(NB)]
        NW = 5 + 2 * CJ + 3 + 4

        def steps(eng, step):
            for s in range(4):
                step(s, s % 2, s < NC_, s >= 1, s >= 2)
            with eng.Fori(2, NC_ // 2 - 1, 1) as i:
                for p in range(2):
                    step(2 * i + p, p, True, True, True)
            for s in range(NC_ - 2, NC_ + 2):
                step(s, s % 2, s < NC_, s < NC_ + 1, True)

        def settle(eng):
            eng.sem_inc(passed, 1)

        def pairs(eng, step):
            for p in range(2):
                step(p, p)
            with eng.Fori(1, NC_ // 2, 1) as i:
                for p in range(2):
                    step(2 * i + p, p)

        def tiles(eng, step):
            for k in range(NB):
                step(k, k, min(k, 2), True)
            with eng.Fori(1, NT // NB, 1) as i:
                for q in range(NB):
                    step(NB * i + q, q, 2, True)
            for k in range(NT, NT + 2):
                step(k, k % NB, 3 if k > NT else 2, False)

        block = es.enter_context(nc.Block())

        @block.sync
        def _(sp):
            sp.wait_ge(memset_done, 1)
            sp.dma_start(wq[:, :], W_q).then_inc(w_in, 16)
            sp.dma_start(wk[:, :], W_k).then_inc(w_in, 16)
            sp.dma_start(wv[:, :], W_v).then_inc(w_in, 16)
            sp.dma_start(bkrow[:, :, :, 0:DK], b_k.rearrange("(o g h d) -> o g h d", o=1, g=G, h=GH)).then_inc(w_in, 16)
            sp.dma_start(bq[:, :], b_q.rearrange("(p o) -> p o", o=1)).then_inc(w_in, 16)
            for b in range(2):
                for j in range(CJ):
                    r = 32 * j + HR * b
                    sp.dma_start(wo[r:r + DK, b], W_o.rearrange("(j g d) n -> j d g n", j=CJ, g=4)[j]).then_inc(w_in, 16)
            sp.dma_start(bv[:, :], b_v.rearrange("(o n) -> o n", o=1).to_broadcast([P, D])).then_inc(w_in, 16)
            sp.dma_start(bo[:, :], b_o.rearrange("(o n) -> o n", o=1).to_broadcast([P, D])).then_inc(w_in, 16)
            sp.dma_start(gx[:, :], g_xattn.rearrange("(o n) -> o n", o=1).to_broadcast([P, 1])).then_inc(w_in, 16)
            sp.dma_start(gf[:, :], g_ffn.rearrange("(o n) -> o n", o=1).to_broadcast([P, 1])).then_inc(w_in, 16)
            sp.dma_start(wred[:, :], w_red).then_inc(w_in, 16)
            sp.dma_start(wgs[:, :], wg).then_inc(w_in, 16)
            sp.dma_start(b1s[:, :], b1.rearrange("e (m p) -> (e m) p", m=HH)).then_inc(w_in, 16)
            for c in range(2):
                sp.dma_start(XC[c][:, :, :], x_t[:, CU * c:CU * c + CU]).then_inc(x_in[c], 16)
                sp.dma_start(C[c][:, :, :], c_t[:, CU * c:CU * c + CU]).then_inc(c_in[c], 16)

            def step(s, p, proj, peak, attend):
                if peak:
                    c, q = s - 1, 1 - p
                    sp.wait_ge(q_sb, c + 1)
                    if s == 1 if isinstance(s, int) else False:
                        sp.wait_ge(setup_v, 2)
                    if not isinstance(s, int) or s >= 3:
                        sp.wait_ge(s2_ps, 2 * CU * (s - 2))
                    for h in range(H):
                        sp.dma_start(Qd[q][HR * (h % GH):HR * (h % GH) + DK, h // GH, h % GH, :],
                                     qT[q][DK * h:DK * h + DK, :]).then_inc(qd_in[q], 16)
                if not isinstance(s, int) or s + 2 < NC_:
                    sp.wait_ge(cT_ps, s + 1)
                    cu = bass.ds(CU * (s + 2), CU)
                    sp.wait_ge(xb_ok, s + 1)
                    sp.dma_start(XC[p][:, :, :], x_t[:, cu]).then_inc(x_in[p], 16)
                    sp.dma_start(C[p][:, :, :], c_t[:, cu]).then_inc(c_in[p], 16)
                if peak:
                    sp.wait_ge(mT_sb, s)
                    for h in range(H):
                        r = HR * (h % GH) + DK
                        sp.dma_start(Qd[q][r:r + 1, h // GH, h % GH, :],
                                     mT[q][h:h + 1, :]).then_inc(qd_in[q], 16)
                if proj:
                    if isinstance(s, int) and s == 0:
                        sp.wait_ge(memset_done, 2)
                    if not isinstance(s, int) or s >= 2:
                        sp.wait_ge(s1_ps, 2 * CU * (s - 1))
                    sp.wait_ge(kb_ok, s + 1)
                    for h in range(H):
                        r = HR * (h % GH)
                        sp.dma_start(Kd[p][DK * h:DK * h + DK, h, :],
                                     kb[r:r + DK, h // GH, :]).then_inc(kd_in[p], 16)
            steps(sp, step)
            sp.wait_ge(s1_ps, 2 * NU)
            sp.dma_start(w1[:, :, :], W1.rearrange("e c h -> c e h")).then_inc(we_in, 16)
            for e in range(NE):
                sp.dma_start(w2[:, e], W2.rearrange("e (m p) c -> e p m c", m=HH)[e]).then_inc(we_in, 16)
            sp.dma_start(kd1[:, 0:NE * D],
                         b2.rearrange("(o e) c -> o (e c)", o=1).to_broadcast([P, NE * D])).then_inc(we_in, 16)
            sp.wait_ge(rec_out, 16 * NU)
            sp.wait_ge(g_lgv, NC_)

            def load(i, q):
                if not isinstance(i, int):
                    sp.wait_ge(scat[q], 4 * (i - q))
                sp.dma_start(rr[q], records[bass.ds(P * i, P), :]).then_inc(r_in[q], 16)
            for q in range(NB):
                load(q, q)
            with sp.Fori(1, NT // NB, 1) as k:
                for q in range(NB):
                    load(NB * k + q, q)
            for q in range(NB):
                sp.wait_ge(scat[q], 16 * (NT // NB))

        @block.gpsimd
        def _(pool):
            nc.gpsimd.memset(bkrow[:, :, :, :], 0.0).then_inc(pool_step, 1)
            nc.gpsimd.memset(one[:, :], 1.0)
            nc.gpsimd.memset(mhalf[:, :], -0.5)
            nc.gpsimd.memset(wo[:, :, :, :], 0.0)
            pool.wait_ge(pool_step, 1)
            nc.gpsimd.memset(bkrow[:, :, :, DK:DK + 1], 1.0).then_inc(memset_done, 1)
            nc.gpsimd.memset(ident[:, :], 0.0).then_inc(pool_step, 1)
            pool.wait_ge(pool_step, 2)
            nc.gpsimd.affine_select(out=ident[:, :], in_=ident[:, :], compare_op=ALU.not_equal, fill=1.0, base=0,
                                    pattern=[[-1, P]], channel_multiplier=1).then_inc(setup_p, 1)
            nc.gpsimd.memset(V[0][:, :, :, :], 0.0)
            nc.gpsimd.memset(V[1][:, :, :, :], 0.0).then_inc(setup_p, 1)
            nc.gpsimd.memset(Kd[0][:, :, :].bitcast(U32), 0)
            nc.gpsimd.memset(Kd[1][:, :, :].bitcast(U32), 0).then_inc(memset_done, 1)
            nc.gpsimd.memset(tri[:, :], 1.0)
            nc.gpsimd.memset(ones[:, :], 1.0)
            nc.gpsimd.memset(blank[:, :], 0.0)
            for e in range(NE):
                nc.gpsimd.memset(rank[:, e:e + 1], float(NE - e))
            nc.gpsimd.iota(tile_i[:, :], pattern=[[1, NT]], base=0, channel_multiplier=0)
            nc.gpsimd.iota(token[:, :], pattern=[[P, NU]], base=0, channel_multiplier=1).then_inc(pchain, 1)
            pool.wait_ge(pchain, 1)
            nc.gpsimd.affine_select(out=tri[:, :], in_=tri[:, :], compare_op=ALU.is_gt, fill=0.0, base=0,
                                    pattern=[[1, P]], channel_multiplier=-1)
            nc.gpsimd.tensor_copy(tile_no[:, :], tile_i[:, :])
            nc.gpsimd.tensor_copy(XR[:, :, R_ID].bitcast(I32), token[:, :])
            nc.gpsimd.memset(blank[:, R_ID:R_ID + 1].bitcast(I32), N).then_inc(pchain, 1)
            pool.wait_ge(pchain, 2)
            pool.dma_start(records.rearrange("(t p) w -> p t w", p=P),
                           blank[:, :].rearrange("p (o w) -> p o w", o=1).to_broadcast([P, NT, RW])).then_inc(fill_ok, 16)
            pool.wait_ge(nrm_ok, 1)
            nc.gpsimd.tensor_tensor(nrm[:, 1:2], nrm[:, 0:1], nrm[:, 3:4], ALU.pow).then_inc(nrm_ok, 1)
            pool.wait_ge(setup_a, 1)
            pool.wait_ge(w_in, 16 * NW)
            nc.gpsimd.tensor_scalar(tgbo[:, :], bo[:, :], tg[:, 0:1], None, ALU.mult).then_inc(pool_step, 1)
            pool.wait_ge(pool_step, 3)

            def norm(c, p):
                pool.wait_ge(stats, c + 1)
                nc.gpsimd.tensor_tensor(rstd[:, :], ve[:, :], mhalf[:, :], ALU.pow).then_inc(rstd_ok, 1)
                pool.wait_ge(rstd_ok, c + 1)
                if not isinstance(c, int) or c >= 1:
                    pool.wait_ge(xT_ps, c)
                settle(pool)
                for u in range(CU):
                    i = nc.gpsimd.tensor_scalar(xn[:, u, :], XC[p][:, u, :],
                                                mv[:, u, 0:1], rstd[:, u:u + 1], ALU.subtract, ALU.mult)
                i.then_inc(xn_ok, 1)
                for u in range(CU):
                    i = nc.gpsimd.tensor_tensor(X[:, bass.ds(CU * c + u, 1), :].rearrange("p o d -> p (o d)"),
                                                XC[p][:, u, :], tgbo[:, :], ALU.add)
                i.then_inc(xb_ok, 1)

            pairs(pool, norm)

            def gate_norm(c, p):
                pool.wait_ge(g_stat, c + 1)
                nc.gpsimd.tensor_tensor(rstd[:, :], ve[:, :], mhalf[:, :], ALU.pow).then_inc(g_rstd, 1)
                pool.wait_ge(g_rstd, c + 1)
                nc.gpsimd.tensor_tensor(shift[:, :], mv[:, :, 0], rstd[:, :], ALU.mult)
                nc.gpsimd.tensor_copy(XR[:, bass.ds(CU * c, CU), R_MEAN], mv[:, :, 0])
                nc.gpsimd.tensor_copy(XR[:, bass.ds(CU * c, CU), R_RSTD], rstd[:, :]).then_inc(g_pay, 1)
                pool.wait_ge(g_pay, 2 * c + 1)
                settle(pool)
                nc.gpsimd.tensor_scalar(shift[:, :], shift[:, :], -1.0, None, ALU.mult).then_inc(g_pay, 1)
            pairs(pool, gate_norm)

            pool.wait_ge(fill_ok, 16)
            pool.wait_ge(pos_ok, 1)
            pool.wait_ge(gate_ok, 1)
            for u in range(NU):
                nc.gpsimd.indirect_dma_start(out=records, out_offset=bass.IndirectOffsetOnAxis(ap=pos[:, u:u + 1], axis=0),
                                             in_=XR[:, u, :], in_offset=None).then_inc(rec_out, 16)

            def stage(i, q):
                p = q % 2
                e = pool.value_load(eid[0:1, bass.ds(i, 1)], min_val=0, max_val=NE - 1)
                if not isinstance(i, int) or i >= 2:
                    pool.wait_ge(f_h, i - 1)
                nc.gpsimd.tensor_copy(w1s[p], w1[:, bass.ds(e, 1), :].rearrange("p o h -> p (o h)")).then_inc(f_w, 1)

            def scatter(i, q):
                pool.wait_ge(f_out, i + 1)
                settle(pool)
                nc.gpsimd.indirect_dma_start(
                    out=out_rows, out_offset=bass.IndirectOffsetOnAxis(ap=rr[q][:, R_ID:R_ID + 1].bitcast(U32), axis=0),
                    in_=fo[q], in_offset=None, bounds_check=N - 1, oob_is_err=False).then_inc(scat[q], 16)
            pool.wait_ge(eid_ok, 1)
            pool.wait_ge(we_in, 16 * (2 + NE))
            def tstep(k, q, head, tail):
                if tail:
                    stage(k, q)
                if head >= 2:
                    scatter(k - 2, (q + 2) % NB)
            tiles(pool, tstep)

        @block.scalar
        def _(act):
            act.wait_ge(w_in, 16 * NW)
            nc.scalar.activation(tg[:, :], gx[:, :], ACT.Tanh).then_inc(setup_a, 1)
            nc.scalar.mul(bqs[:, :], bq[:, :], ISC).then_inc(setup_a, 1)
            act.wait_ge(setup_a, 2)
            act.wait_ge(setup_t, 1)
            nc.scalar.activation(bk16[:, :], m0[:, 0:G], ACT.Copy).then_inc(setup_a, 1)
            act.wait_ge(setup_a, 3)
            nc.scalar.activation(tgf[:, :], gf[:, :], ACT.Tanh).then_inc(setup_a, 1)

            def exp(s, u):
                c = s - 2
                for g in range(G):
                    act.wait_ge(s2_ps, 2 * CU * c + 2 * u + g + 1)
                    if u < 2:
                        if not isinstance(s, int) or s >= 3:
                            act.wait_ge(pv_ps, CU * c + u - 1)
                    else:
                        act.wait_ge(pv_ps, CU * c + u - 1)
                    nc.scalar.activation(PT[u % 2][:, GH * g:GH * g + GH, :], s2p[g][:, :].rearrange("p (h q) -> p h q", h=GH),
                                         ACT.Exp).then_inc(pt_ok, 1)

            def step(s, p, proj, peak, attend):
                if proj:
                    act.wait_ge(xT_ps, s + 1)
                    nc.scalar.activation(xT[:, :], m0[:, :], ACT.Copy).then_inc(xT_sb, 1)
                if attend:
                    exp(s, 0)
                if proj:
                    act.wait_ge(cT_ps, s + 1)
                    nc.scalar.activation(cT[:, :], m1[:, :], ACT.Copy).then_inc(cT_sb, 1)
                if attend:
                    for u in range(1, CU):
                        exp(s, u)
                if peak:
                    act.wait_ge(mT_ps, s)
                    nc.scalar.mul(mT[1 - p][:, :], m0[0:H, :], -1.0).then_inc(mT_sb, 1)
                if proj:
                    act.wait_ge(q_ps, s + 1)
                    nc.scalar.activation(qT[p][:, :], m1[:, :], ACT.Identity, bias=bqs[:, 0:1], scale=ISC).then_inc(q_sb, 1)
                    for g, m in enumerate((m0, m1)):
                        act.wait_ge(k_ps, 2 * s + g + 1)
                        nc.scalar.activation(kT[p][:, g, :], m[:, :], ACT.Identity, bias=bk16[:, g:g + 1]).then_inc(k_sb, 1)
            steps(act, step)

            def gate_xn(c, p):
                act.wait_ge(g_pay, 2 * c + 2)
                if not isinstance(c, int) or c >= 1:
                    act.wait_ge(g_tr, c)
                for u in range(CU):
                    i = nc.scalar.activation(xn[:, u, :], X[:, bass.ds(CU * c + u, 1), :].rearrange("p o d -> p (o d)"),
                                             ACT.Identity, bias=shift[:, u:u + 1], scale=rstd[:, u:u + 1])
                i.then_inc(g_xn, 1)

            def gate_copy(c, p):
                gate_xn(c, p)
                act.wait_ge(g_tr, c + 1)
                if not isinstance(c, int) or c >= 2:
                    act.wait_ge(g_lg, c - 1)
                nc.scalar.activation(gT[p][:, :], s2p[p][:, :], ACT.Copy).then_inc(g_xT, 1)
            pairs(act, gate_copy)
            act.wait_ge(diff_ok, 1)
            nc.scalar.activation(ex, lg, ACT.Exp).then_inc(ex_ok, 1)

            act.wait_ge(eid_ok, 1)
            def tstep(k, q, head, tail):
                if head >= 1 and (tail or k == NT):
                    i, p = k - 1, 1 - q % 2
                    e = act.value_load(eid[0:1, bass.ds(i, 1)], min_val=0, max_val=NE - 1)
                    act.wait_ge(f_h, i + 1)
                    if not isinstance(i, int) or i >= 2:
                        act.wait_ge(f_o, i - 1)
                    for m in range(HH):
                        a = nc.scalar.activation(fh[p][:, m, :], s1p[p][:, P * m:P * m + P], ACT.Gelu,
                                                 bias=b1c[:, bass.ds(e, 1), m])
                    a.then_inc(f_g, 1)
            tiles(act, tstep)

        @block.vector
        def _(dve):
            nc.vector.memset(ksum[:, :], 0.0).then_inc(setup_v, 1)
            dve.wait_ge(setup_v, 1)
            nc.vector.memset(ksum[0:S, 0:HR], 1.0)
            nc.vector.memset(ksum[S:P, HR:2 * HR], 1.0)
            nc.vector.memset(Qd[0][:, :, :, :], 0.0)
            nc.vector.memset(Qd[1][:, :, :, :], 0.0)
            nc.vector.memset(wk16[:, :, :, :], 0.0).then_inc(setup_v, 1)
            dve.wait_ge(setup_v, 2)
            dve.wait_ge(w_in, 16 * NW)
            nc.vector.tensor_copy(wk16[:, :, :, 0:DK], wk[:, :].rearrange("p (g h d) -> p g h d", g=G, h=GH)).then_inc(setup_v, 1)

            def stat(c, p):
                dve.wait_ge(x_in[p], 16 * (c // 2) + 16 if isinstance(c, int) else 8 * (c - p) + 16)
                if not isinstance(c, int) or c >= 1:
                    dve.wait_ge(xn_ok, c)
                for u in range(CU):
                    i = nc.vector.bn_stats(st[:, u, :], XC[p][:, u, :])
                i.then_inc(stat_step, 1)
                dve.wait_ge(stat_step, 2 * c + 1)
                settle(dve)
                for u in range(CU):
                    i = nc.vector.bn_aggr(mv[:, u, :], st[:, u, :])
                i.then_inc(stat_step, 1)
                dve.wait_ge(stat_step, 2 * c + 2)
                nc.vector.tensor_scalar_add(ve[:, :], mv[:, :, 1], EPS).then_inc(stats, 1)

            def peak_of(s, u):
                for g in range(G):
                    dve.wait_ge(s1_ps, 2 * CU * (s - 1) + 2 * u + g + 1)
                    if u == 0 and g == 0 and (not isinstance(s, int) or s >= 2):
                        dve.wait_ge(mT_ps, s - 1)
                    nc.vector.tensor_reduce(mx[:, u, GH * g:GH * g + GH], s1p[g][:, :].rearrange("p (h k) -> p h k", h=GH),
                                            AX_X, ALU.max).then_inc(mx_ok, 1)

            def norm_of(s, u):
                n = CU * (s - 2) + u
                dve.wait_ge(pv_ps, n + 1)
                nc.vector.reciprocal(rec[:, :], pvp[:, CJ * S:2 * CJ * S]).then_inc(rec_ok, 1)
                dve.wait_ge(rec_ok, n + 1)
                if u >= 2 or not isinstance(s, int) or s >= 3:
                    dve.wait_ge(o_ps, n - 1)
                nc.vector.tensor_tensor(OT[u % 2][:, :, :].rearrange("p g q -> p (g q)"), pvp[:, 0:CJ * S], rec[:, :],
                                        ALU.mult).then_inc(ot_ok, 1)

            def x1_of(s, u):
                n = CU * (s - 2) + u
                dve.wait_ge(o_ps, n + 1)
                dve.wait_ge(xb_ok, s - 1)
                xu = X[:, bass.ds(n, 1), :].rearrange("p o d -> p (o d)")
                nc.vector.scalar_tensor_tensor(out=xu, in0=m2[:, 0:D], scalar=tg[:, 0:1], in1=xu,
                                               op0=ALU.mult, op1=ALU.add).then_inc(x1_ok, 1)

            vc = [0]

            def link(i):
                vc[0] += 1
                i.then_inc(chain, 1)
                dve.wait_ge(chain, vc[0])

            nc.vector.memset(nrm[:, 3:4], 0.5)
            link(nc.vector.tensor_tensor(wg2[:, :], wgs[:, :], wgs[:, :], ALU.mult))
            nc.vector.tensor_reduce(nrm[:, 0:1], wg2[:, :], AX_X, ALU.add).then_inc(nrm_ok, 1)
            dve.wait_ge(nrm_ok, 2)
            link(nc.vector.tensor_scalar_max(nrm[:, 2:3], nrm[:, 1:2], 1e-4))
            link(nc.vector.reciprocal(nrm[:, 0:1], nrm[:, 2:3]))
            nc.vector.tensor_scalar(wgn[:, :], wgs[:, :], nrm[:, 0:1], None, ALU.mult).then_inc(wgn_ok, 1)
            dve.wait_ge(setup_t, 2)
            nc.vector.tensor_copy(b1c[:, :, :].rearrange("p e m -> p (e m)"), s1p[0][:, 0:NE * HH])
            nc.vector.tensor_copy(wredT[:, :], m1[0:GD, 0:P]).then_inc(wgT_ok, 1)
            dve.wait_ge(setup_t, 3)
            nc.vector.tensor_copy(wgT[:, :], m2[0:GD, 0:NE]).then_inc(wgT_ok, 1)
            dve.wait_ge(setup_t, 4)
            nc.vector.tensor_copy(wc[:, :], pvp[:, 0:NE]).then_inc(wc_ok, 1)

            stat(0, 0)

            def step(s, p, proj, peak, attend):
                for u in range(CU):
                    if peak:
                        peak_of(s, u)
                    if attend:
                        norm_of(s, u) if u < CU - 1 else None
                        if u >= 1:
                            x1_of(s, u - 1) if u < CU - 1 else None
                if attend:
                    norm_of(s, 3)
                    x1_of(s, 2)
                if proj:
                    dve.wait_ge(q_sb, s + 1)
                    nc.vector.tensor_copy(qb[:, :], qT[p][:, :]).then_inc(qb_ok, 1)
                    if not isinstance(s, int) or s >= 1:
                        dve.wait_ge(kd_in[1 - p], 256 * ((s + 1) // 2) if isinstance(s, int) else 128 * (s + p))
                    for g in range(G):
                        dve.wait_ge(k_sb, 2 * s + g + 1)
                        i = nc.vector.tensor_copy(kb[:, g, :], kT[p][:, g, :])
                    i.then_inc(kb_ok, 1)
                if attend:
                    x1_of(s, 3)
                if proj:
                    dve.wait_ge(v_ps, s + 1)
                    if isinstance(s, int) and s < 2:
                        dve.wait_ge(setup_p, 2)
                    for b in range(2):
                        r = slice(S * b, S * b + S)
                        i = nc.vector.tensor_tensor(
                            V[p][r, :, :, HR * b:HR * b + DK],
                            m2[r, :].rearrange("p (u h d) -> p u h d", u=CU, h=H),
                            bv[r, :].rearrange("p (o h d) -> p o h d", o=1, h=H).to_broadcast([S, CU, H, DK]), ALU.add)
                    i.then_inc(v_sb, 1)
                    if not isinstance(s, int) or s + 1 < NC_:
                        stat(s + 1, 1 - p)
            steps(dve, step)

            def gate_stat(c, p):
                if not isinstance(c, int) or c >= 1:
                    dve.wait_ge(g_xn, c)
                else:
                    dve.wait_ge(x1_ok, NU)
                for u in range(CU):
                    i = nc.vector.bn_stats(st[:, u, :], X[:, bass.ds(CU * c + u, 1), :].rearrange("p o d -> p (o d)"))
                i.then_inc(gs1, 1)
                dve.wait_ge(gs1, 2 * c + 1)
                settle(dve)
                for u in range(CU):
                    i = nc.vector.bn_aggr(mv[:, u, :], st[:, u, :])
                i.then_inc(gs1, 1)
                dve.wait_ge(gs1, 2 * c + 2)
                nc.vector.tensor_scalar_add(ve[:, :], mv[:, :, 1], EPS).then_inc(g_stat, 1)

            def gate_keep(c, p):
                dve.wait_ge(g_lg, c + 1)
                nc.vector.tensor_copy(lg[:, bass.ds(CU * c, CU), :],
                                      s1p[p][:, 0:CU * NE].rearrange("p (u e) -> p u e", e=NE)).then_inc(g_lgv, 1)

            def gate(c, p):
                gate_stat(c, p)
                if not isinstance(c, int) or c >= 1:
                    gate_keep(c - 1, 1 - p)
            pairs(dve, gate)
            gate_keep(NC_ - 1, 1)
            dve.wait_ge(g_lgv, NC_)

            def col(a, n=1):
                return small[:, a * NU:a * NU + n * NU]

            def wide(ap):
                return ap.rearrange("p (u o) -> p u o", o=1).to_broadcast([P, NU, NE])

            def per_expert(ap):
                return ap.rearrange("p (o e) -> p o e", o=1).to_broadcast([P, NU, NE])

            link(nc.vector.tensor_reduce(col(0), lg, AX_X, ALU.max))
            nc.vector.tensor_tensor(lg, lg, wide(col(0)), ALU.subtract).then_inc(diff_ok, 1)
            dve.wait_ge(ex_ok, 1)
            nc.vector.tensor_reduce(col(1), ex, AX_X, ALU.add)
            link(nc.vector.tensor_reduce(col(2), ex, AX_X, ALU.max))
            link(nc.vector.reciprocal(col(3), col(1)))
            link(nc.vector.tensor_tensor(col(4), col(2), col(3), ALU.mult))
            dve.wait_ge(setup_a, 4)
            nc.vector.tensor_scalar(XR[:, :, R_GATE], col(4), tgf[:, 0:1], None, ALU.mult).then_inc(gate_ok, 1)
            link(nc.vector.tensor_tensor(ky, ex, wide(col(2)), ALU.is_equal))
            link(nc.vector.tensor_tensor(ky, ky, per_expert(rank[:, :]), ALU.mult))
            link(nc.vector.tensor_reduce(col(5), ky, AX_X, ALU.max))
            nc.vector.tensor_tensor(oh[:, :, :], ky, wide(col(5)), ALU.is_equal).then_inc(oh_ok, 1)
            dve.wait_ge(cnt_ps, 2)
            nc.vector.tensor_copy(tot, m1[:, :].rearrange("p (u e) -> p u e", e=NE))
            link(nc.vector.tensor_copy(ta, m1[:, :].rearrange("p (u e) -> p u e", e=NE)))
            a, b, k = ta, tb, 1
            while k < NU:
                nc.vector.tensor_copy(b[:, 0:k, :], a[:, 0:k, :])
                link(nc.vector.tensor_tensor(b[:, k:NU, :], a[:, k:NU, :], a[:, 0:NU - k, :], ALU.add))
                a, b, k = b, a, 2 * k
            tl = lambda n: col(6 + n)[:, 0:NE]
            link(nc.vector.tensor_scalar_add(tl(0).bitcast(I32), a[:, NU - 1, :], float(P - 1)))
            link(nc.vector.tensor_single_scalar(tl(1).bitcast(I32), tl(0).bitcast(I32), 7, ALU.arith_shift_right))
            nc.vector.tensor_copy(tl(2), tl(1).bitcast(I32))
            link(nc.vector.tensor_copy(tl(3), tl(1).bitcast(I32)))
            c, d, k = 3, 4, 1
            while k < NE:
                nc.vector.tensor_copy(tl(d)[:, 0:k], tl(c)[:, 0:k])
                link(nc.vector.tensor_tensor(tl(d)[:, k:NE], tl(c)[:, k:NE], tl(c)[:, 0:NE - k], ALU.add))
                c, d, k = d, c, 2 * k
            link(nc.vector.tensor_tensor(tl(5), tl(c), tl(2), ALU.subtract))
            link(nc.vector.tensor_scalar_mul(tl(5), tl(5), float(P)))
            link(nc.vector.tensor_tensor(b, a, tot, ALU.subtract))
            link(nc.vector.tensor_tensor(b, b, per_expert(tl(5)), ALU.add))
            link(nc.vector.tensor_tensor(b, m0[:, :].rearrange("p (u e) -> p u e", e=NE), b, ALU.add))
            link(nc.vector.tensor_tensor(b, b, oh[:, :, :], ALU.mult))
            link(nc.vector.tensor_reduce(col(1), b, AX_X, ALU.add))
            nc.vector.tensor_copy(pos[:, :], col(1)).then_inc(pos_ok, 1)
            link(nc.vector.tensor_tensor(
                cmpt, tl(c).rearrange("p (o e) -> p o e", o=1).to_broadcast([P, NT, NE]),
                tile_no[:, :].rearrange("p (t o) -> p t o", o=1).to_broadcast([P, NT, NE]), ALU.is_le))
            cnt = Qd[1][:, 0, 2, 0:NT]
            link(nc.vector.tensor_reduce(cnt, cmpt, AX_X, ALU.add))
            nc.vector.tensor_scalar_min(eid[:, :], cnt, float(NE - 1)).then_inc(eid_ok, 1)
            dve.wait_ge(eid_ok, 1)
            dve.wait_ge(we_in, 16 * (2 + NE))

            def ft_norm(i, q):
                p = q % 2
                if isinstance(i, int):
                    dve.wait_ge(r_in[q], 16 * (i // NB) + 16)
                else:
                    dve.wait_ge(r_in[q], 4 * (i - q) + 16)
                if not isinstance(i, int) or i >= 2:
                    dve.wait_ge(f_tr, i - 1)
                nc.vector.tensor_scalar(fx[p], rr[q][:, 0:D], rr[q][:, R_MEAN:R_MEAN + 1], rr[q][:, R_RSTD:R_RSTD + 1],
                                        ALU.subtract, ALU.mult).then_inc(f_xn, 1)

            def ft_copy(i, q):
                p = q % 2
                dve.wait_ge(f_tr, i + 1)
                if not isinstance(i, int) or i >= 2:
                    dve.wait_ge(f_h, i - 1)
                nc.vector.tensor_copy(fxT[p], s2p[p][:, 0:P]).then_inc(f_xT, 1)

            def ft_out(i, q):
                p = q % 2
                e = dve.value_load(eid[0:1, bass.ds(i, 1)], min_val=0, max_val=NE - 1)
                dve.wait_ge(f_o, i + 1)
                nc.vector.tensor_tensor(ft[p], (m0, m1)[p][:, 0:D], b2r[:, bass.ds(e, 1), :].rearrange("p o c -> p (o c)"),
                                        ALU.add).then_inc(f_t, 1)
                dve.wait_ge(f_t, i + 1)
                if not isinstance(i, int) or i >= NB:
                    dve.wait_ge(scat[q], 4 * (i - q))
                nc.vector.scalar_tensor_tensor(out=fo[q], in0=ft[p], scalar=rr[q][:, R_GATE:R_GATE + 1],
                                               in1=rr[q][:, 0:D], op0=ALU.mult, op1=ALU.add).then_inc(f_out, 1)

            ft_norm(0, 0)

            def tstep(k, q, head, tail):
                if tail and (not isinstance(k, int) or k + 1 < NT):
                    if isinstance(k, int):
                        ft_norm(k + 1, (q + 1) % NB)
                if tail:
                    ft_copy(k, q)
                if head >= 2:
                    ft_out(k - 2, (q + 2) % NB)
            for k in range(NB):
                ft_norm(k + 1, (k + 1) % NB)
                ft_copy(k, k)
                if k >= 2:
                    ft_out(k - 2, k - 2)
            with dve.Fori(1, NT // NB - 1, 1) as i:
                for q in range(NB):
                    ft_norm(NB * i + q + 1, (q + 1) % NB)
                    ft_copy(NB * i + q, q)
                    ft_out(NB * i + q - 2, (q + 2) % NB)
            for k in range(NT - NB, NT + 2):
                if k + 1 < NT:
                    ft_norm(k + 1, (k + 1) % NB)
                if k < NT:
                    ft_copy(k, k % NB)
                ft_out(k - 2, (k - 2) % NB)

        @block.tensor
        def _(pe):
            pe.wait_ge(setup_p, 1)
            pe.wait_ge(w_in, 16 * NW)
            for g in range(G):
                i = nc.tensor.matmul(m0[:, g:g + 1], bkrow[0:1, g].rearrange("p h r -> p (h r)"), one[0:1, 0:1],
                                     start=(g == 0), stop=True, skip_group_check=True)
            i.then_inc(setup_t, 1)
            nc.tensor.transpose(s1p[0][:, 0:NE * HH], b1s[:, :], ident[0:NE * HH, 0:NE * HH])
            nc.tensor.transpose(m1[0:GD, 0:P], wred[:, :], ident[:, :]).then_inc(setup_t, 1)
            pe.wait_ge(wgn_ok, 1)
            nc.tensor.transpose(m2[0:GD, 0:NE], wgn[:, :], ident[0:NE, 0:NE]).then_inc(setup_t, 1)
            pe.wait_ge(wgT_ok, 2)
            nc.tensor.matmul(pvp[:, 0:NE], wredT[:, :], wgT[:, :], start=True, stop=True).then_inc(setup_t, 1)
            pe.wait_ge(wc_ok, 1)
            pe.wait_ge(setup_a, 3)
            pe.wait_ge(setup_v, 3)

            def scores2(s, u, p):
                for g in range(G):
                    n = 2 * CU * (s - 2) + 2 * u + g
                    if u or not isinstance(s, int) or s >= 3:
                        pe.wait_ge(pt_ok, n - 1)
                    for b in range(2):
                        t = slice(UNIT * u + S * b, UNIT * u + S * b + S)
                        i = nc.tensor.matmul(s2p[g][S * b:S * b + S, :].rearrange("p (h q) -> p h q", h=GH),
                                             kT[p][:, g, t], Qd[p][:, g, :, t], start=True, stop=True)
                    i.then_inc(s2_ps, 1)

            def scores1(s, u, p):
                for g in range(G):
                    n = 2 * CU * (s - 1) + 2 * u + g
                    if u or not isinstance(s, int) or s >= 2:
                        pe.wait_ge(mx_ok, n - 1)
                    for b in range(2):
                        t = slice(UNIT * u + S * b, UNIT * u + S * b + S)
                        i = nc.tensor.matmul(s1p[g][S * b:S * b + S, :].rearrange("p (h q) -> p h q", h=GH),
                                             qb[:, t], Kd[p][:, GH * g:GH * g + GH, t], start=True, stop=True)
                    i.then_inc(s1_ps, 1)

            def values(s, u, p):
                n = CU * (s - 2) + u
                pe.wait_ge(pt_ok, 2 * n + 2)
                if u or not isinstance(s, int) or s >= 3:
                    pe.wait_ge(ot_ok, n)
                for j in range(CJ):
                    nc.tensor.matmul(pvp[32 * j:32 * j + 32, CJ * S:2 * CJ * S], ksum[:, :],
                                     PT[u % 2][:, 4 * j:4 * j + 4, :].rearrange("p h q -> p (h q)"),
                                     start=True, stop=False, skip_group_check=True)
                for g in range(4):
                    for j in range(CJ):
                        i = nc.tensor.matmul(pvp[32 * j:32 * j + 32, S * g:S * g + S], V[p][:, u, 4 * j + g, :],
                                             PT[u % 2][:, 4 * j + g, :], start=False, stop=(g == 3), skip_group_check=True)
                i.then_inc(pv_ps, 1)

            def project_out(s, u):
                n = CU * (s - 2) + u
                pe.wait_ge(ot_ok, n + 1)
                if u:
                    pe.wait_ge(x1_ok, n)
                elif not isinstance(s, int):
                    pe.wait_ge(v_sb, s)
                else:
                    pe.wait_ge(v_sb, min(s, NC_))
                for g in range(4):
                    for b in range(2):
                        i = nc.tensor.matmul(m2[S * b:S * b + S, 0:D], OT[u % 2][:, g, :], wo[:, b, g, :],
                                             start=(g == 0), stop=(g == 3), skip_group_check=True)
                i.then_inc(o_ps, 1)

            def step(s, p, proj, peak, attend):
                if proj:
                    pe.wait_ge(xn_ok, s + 1)
                    if not isinstance(s, int) or s >= 1:
                        pe.wait_ge(k_sb, 2 * s)
                    for u in range(CU):
                        i = nc.tensor.transpose(m0[:, UNIT * u:UNIT * u + UNIT], xn[:, u, :], ident[:, :])
                    i.then_inc(xT_ps, 1)
                if attend:
                    pe.wait_ge(qd_in[p], 512 * (s // 2) if isinstance(s, int) else 256 * (s - p))
                    scores2(s, 0, p)
                if proj:
                    pe.wait_ge(c_in[p], 16 * (s // 2) + 16 if isinstance(s, int) else 8 * (s - p) + 16)
                    for u in range(CU):
                        i = nc.tensor.transpose(m1[:, UNIT * u:UNIT * u + UNIT], C[p][:, u, :], ident[:, :])
                    i.then_inc(cT_ps, 1)
                for u in range(CU):
                    if attend and u:
                        scores2(s, u, p)
                    if attend and u:
                        values(s, u - 1, p)
                    if peak:
                        if u == 0:
                            q = 1 - p
                            pe.wait_ge(qb_ok, s)
                            pe.wait_ge(kd_in[q], 256 * ((s + 1) // 2) if isinstance(s, int) else 128 * (s + p))
                        scores1(s, u, 1 - p)
                    if attend and u >= 2:
                        project_out(s, u - 2)
                if attend:
                    values(s, 3, p)
                    project_out(s, 2)
                if peak:
                    pe.wait_ge(mx_ok, 2 * CU * s)
                    if proj:
                        pe.wait_ge(xT_sb, s + 1)
                    for u in range(CU):
                        i = nc.tensor.transpose(m0[0:H, UNIT * u:UNIT * u + UNIT], mx[:, u, :], ident[:, :])
                    i.then_inc(mT_ps, 1)
                if proj:
                    pe.wait_ge(xT_sb, s + 1)
                    pe.wait_ge(cT_sb, s + 1)
                    nc.tensor.matmul(m1[:, :], wq[:, :], xT[:, :], start=True, stop=True).then_inc(q_ps, 1)
                if attend:
                    project_out(s, 3)
                if proj:
                    if peak:
                        pe.wait_ge(mT_sb, s)
                    nc.tensor.matmul(m0[:, :], wk16[:, 0].rearrange("p h r -> p (h r)"), cT[:, :], start=True,
                                     stop=True).then_inc(k_ps, 1)
                    pe.wait_ge(q_sb, s + 1)
                    nc.tensor.matmul(m1[:, :], wk16[:, 1].rearrange("p h r -> p (h r)"), cT[:, :], start=True,
                                     stop=True).then_inc(k_ps, 1)
                    if attend:
                        pe.wait_ge(x1_ok, CU * (s - 1))
                    elif not isinstance(s, int) or s >= 1:
                        pe.wait_ge(v_sb, s)
                    for u in range(CU):
                        i = nc.tensor.matmul(m2[:, D * u:D * u + D], cT[:, UNIT * u:UNIT * u + UNIT], wv[:, :],
                                             start=(u == 0), stop=(u == CU - 1), skip_group_check=True)
                    i.then_inc(v_ps, 1)
            steps(pe, step)

            def gate_logits(c, p):
                pe.wait_ge(g_xT, c + 1)
                if isinstance(c, int) and c < 2:
                    pe.wait_ge(mx_ok, 2 * NU)
                else:
                    pe.wait_ge(g_lgv, c - 1)
                for u in range(CU):
                    i = nc.tensor.matmul(s1p[p][:, NE * u:NE * u + NE], gT[p][:, UNIT * u:UNIT * u + UNIT], wc[:, :],
                                         start=(u == 0), stop=(u == CU - 1), skip_group_check=True)
                i.then_inc(g_lg, 1)

            def gate_tr(c, p):
                pe.wait_ge(g_xn, c + 1)
                if isinstance(c, int) and c < 2:
                    pe.wait_ge(pt_ok, 2 * NU)
                else:
                    pe.wait_ge(g_xT, c - 1)
                for u in range(CU):
                    i = nc.tensor.transpose(s2p[p][:, UNIT * u:UNIT * u + UNIT], xn[:, u, :], ident[:, :])
                i.then_inc(g_tr, 1)
                if not isinstance(c, int) or c >= 1:
                    gate_logits(c - 1, 1 - p)
            pairs(pe, gate_tr)
            gate_logits(NC_ - 1, 1)
            pe.wait_ge(oh_ok, 1)
            nc.tensor.matmul(m0[:, :], tri[:, :], oh[:, :, :].rearrange("p u e -> p (u e)"), start=True, stop=True).then_inc(cnt_ps, 1)
            nc.tensor.matmul(m1[:, :], ones[:, :], oh[:, :, :].rearrange("p u e -> p (u e)"), start=True, stop=True).then_inc(cnt_ps, 1)

            pe.wait_ge(eid_ok, 1)
            pe.wait_ge(we_in, 16 * (2 + NE))
            def tstep(k, q, head, tail):
                p = q % 2
                if tail:
                    pe.wait_ge(f_xn, k + 1)
                    if not isinstance(k, int) or k >= 2:
                        pe.wait_ge(f_xT, k - 1)
                    nc.tensor.transpose(s2p[p][:, 0:P], fx[p], ident[:, :]).then_inc(f_tr, 1)
                if head >= 1 and (tail or k == NT):
                    i, r = k - 1, 1 - p
                    pe.wait_ge(f_xT, i + 1)
                    pe.wait_ge(f_w, i + 1)
                    if not isinstance(i, int) or i >= 2:
                        pe.wait_ge(f_g, i - 1)
                    for m in range(HH):
                        j = nc.tensor.matmul(s1p[r][:, P * m:P * m + P], w1s[r][:, P * m:P * m + P], fxT[r],
                                             start=(m == 0), stop=(m == HH - 1), skip_group_check=True)
                    j.then_inc(f_h, 1)
                if head >= 2:
                    i = k - 2
                    e = pe.value_load(eid[0:1, bass.ds(i, 1)], min_val=0, max_val=NE - 1)
                    pe.wait_ge(f_g, i + 1)
                    if not isinstance(i, int) or i >= 2:
                        pe.wait_ge(f_t, i - 1)
                    for m in range(HH):
                        j = nc.tensor.matmul((m0, m1)[p][:, 0:D], fh[p][:, m, :],
                                             w2[:, bass.ds(e, 1), m, :].rearrange("p o c -> p (o c)"),
                                             start=(m == 0), stop=(m == HH - 1))
                    j.then_inc(f_o, 1)
            tiles(pe, tstep)


_INS = ["x", "ctx_1024", "g_xattn", "g_ffn", "L0_xattn_W_q", "L0_xattn_b_q", "L0_xattn_W_k", "L0_xattn_b_k",
        "L0_xattn_W_v", "L0_xattn_b_v", "L0_xattn_W_o", "L0_xattn_b_o", "L0_ffn_w_red", "L0_ffn_wg",
        "L0_ffn_W1", "L0_ffn_b1", "L0_ffn_W2", "L0_ffn_b2"]


def kernel(**inputs):
    import numpy as _np
    import concourse.bacc as _bacc
    from concourse import mybir as _mybir
    from concourse.bass_utils import run_bass_kernel_spmd as _run

    nc = _bacc.Bacc("TRN2", target_bir_lowering=False, num_devices=1)
    arrays, args = {}, []
    for name in _INS:
        a = _np.ascontiguousarray(inputs[name])
        arrays[f"in_{name}"] = a
        args.append(nc.dram_tensor(f"in_{name}", a.shape, _mybir.dt.from_np(a.dtype), kind="ExternalInput").ap())
    args.append(nc.dram_tensor("out_0", (B, S, D), F32, kind="ExternalOutput").ap())
    gated_block(nc, *args)
    r = _run(nc, [arrays], core_ids=[0])
    return r.results[0]["out_0"]
```

```python
from contextlib import ExitStack

import concourse.bass as bass
from concourse import mybir

ALU = mybir.AluOpType
ACT = mybir.ActivationFunctionType
F32 = mybir.dt.float32
BF16 = mybir.dt.bfloat16
U32 = mybir.dt.uint32
I32 = mybir.dt.int32
AX_X = mybir.AxisListType.X

P = 128
D = 128
H = 16
DK = D // H
S = 64
B = 128
N = B * S
UNIT = P
CU = 4
CT = CU * UNIT
NC_ = N // CT
NU = N // UNIT
GH = 8
G = H // GH
HR = P // GH
CJ = 4
EPS = 1e-5
ISC = float(DK) ** -0.5
NE = 8
GD = 16
HID = 256
HH = HID // P
NT = N // P + NE
RW = D + 4
R_RSTD, R_MEAN, R_GATE, R_ID = D, D + 1, D + 2, D + 3
NB = 8


def gated_block(nc, x, ctx_in, g_xattn, g_ffn, W_q, b_q, W_k, b_k, W_v, b_v, W_o, b_o, w_red, wg, W1, b1, W2, b2, out):
    es = ExitStack()
    with es:
        def sb(name, shape, dt=F32):
            return es.enter_context(nc.sbuf_tensor(name, shape, dt))

        def pb(name, shape, dt=F32):
            return es.enter_context(nc.psum_tensor(name, shape, dt))

        def sem(name):
            return es.enter_context(nc.semaphore(name))

        x_t = x.rearrange("(t two) s d -> (two s) t d", two=2)
        c_t = ctx_in.rearrange("(t two) s d -> (two s) t d", two=2)
        out_rows = out.rearrange("b s d -> (b s) d")
        records = nc.dram_tensor("records", [NT * P, RW], F32, kind="Internal").ap()

        ident = sb("ident", [P, P])
        w16 = sb("w16", [P, 2, G, GH, HR])
        wv = sb("wv", [P, D])
        wo = sb("wo", [P, 2, CJ, D])
        b16 = sb("b16", [P, 2, G])
        hmask = sb("hmask", [P, GH])
        one = sb("one", [1, 1])
        bv = sb("bv", [P, D])
        tgbo = sb("tgbo", [P, D])
        gx = sb("gx", [P, 1])
        tg = sb("tg", [P, 1])
        ksum = sb("ksum", [P, 32])
        mhalf = sb("mhalf", [P, CU])
        tri = sb("tri", [P, P], BF16)
        ones = sb("ones", [P, P], BF16)
        rank = sb("rank", [P, NE])
        tile_no = sb("tile_no", [P, NT])
        blank = sb("blank", [P, RW])
        tgf = sb("tgf", [P, 1])
        gf = sb("gf", [P, 1])
        wred = sb("wred", [P, GD])
        wredT = sb("wredT", [GD, P])
        wgs = sb("wgs", [NE, GD])
        wg2 = sb("wg2", [NE, GD])
        wgn = sb("wgn", [NE, GD])
        wgT = sb("wgT", [GD, NE])
        nrm = sb("nrm", [NE, 4])
        wc = sb("wc", [P, NE])
        b1c = sb("b1c", [P, NE, HH])
        eid = sb("eid", [P, NT], I32)
        pos = sb("pos", [P, NU], U32)
        XR = sb("XR", [P, NU, RW])
        X = XR[:, :, 0:D]
        XC = [sb(f"XC{i}", [P, CU, D]) for i in range(2)]
        C = [sb(f"C{i}", [P, CU, D]) for i in range(2)]
        st = sb("st", [P, CU, 6])
        mv = sb("mv", [P, CU, 2])
        ve = sb("ve", [P, CU])
        rstd = sb("rstd", [P, CU])
        gst = sb("gst", [P, CU, 6])
        gmv = sb("gmv", [P, CU, 2])
        gve = sb("gve", [P, CU])
        grstd = sb("grstd", [P, CU])
        wmean = sb("wmean", [GD, 2])
        lg = sb("lg", [P, NU, NE])
        xn = sb("xn", [P, CU, D])
        xT = sb("xT", [P, CT])
        cT = sb("cT", [P, CT])
        Q16 = [sb(f"Q16{i}", [P, G, CT]) for i in range(2)]
        qb = sb("qb", [P, G, CT], BF16)
        kT = [sb(f"kT{i}", [P, G, CT]) for i in range(2)]
        kb = sb("kb", [P, G, CT], BF16)
        Kd = [sb(f"Kd{i}", [P, G, GH, CT], BF16) for i in range(2)]
        Qd = [sb(f"Qd{i}", [P, G, GH, CT]) for i in range(2)]
        V = [sb(f"V{i}", [P, CU, H, 32]) for i in range(2)]
        mx = sb("mx", [P, CU, G, GH, HR])
        PT = [sb(f"PT{i}", [P, H, S]) for i in range(2)]
        rec = sb("rec", [P, CJ * S])
        OT = [sb(f"OT{i}", [P, CJ, S]) for i in range(2)]

        ex, ky, ta = (V[0][:, i].rearrange("p h r -> p (h r)").rearrange("p (u e) -> p u e", e=NE) for i in range(3))
        tb, tot = (V[1][:, i].rearrange("p h r -> p (h r)").rearrange("p (u e) -> p u e", e=NE) for i in range(2))
        wq, wk, bo, b1s = (PT[0][:, 2 * i:2 * i + 2, :].rearrange("p h q -> p (h q)") for i in range(4))
        b1s = b1s[0:NE * HH, :]
        tile_i, token = eid, pos[:, :].bitcast(I32)
        brow = PT[1][0:1, 0:2 * G * P // S, :].rearrange("p h q -> p (h q)").rearrange("p (i g h r) -> p i g h r", i=2, g=G, h=GH)
        small = PT[0][:, :, :].rearrange("p h q -> p (h q)")
        kd0 = Kd[0][:, :, :, :].rearrange("p g h t -> p (g h t)").bitcast(F32)
        kd1 = Kd[1][:, :, :, :].rearrange("p g h t -> p (g h t)").bitcast(F32)
        w1 = kd0[:, 0:NE * HID].rearrange("p (e h) -> p e h", e=NE)
        w2 = kd0[:, NE * HID:2 * NE * HID].rearrange("p (e m c) -> p e m c", e=NE, m=HH)
        b2r = kd1[:, 0:NE * D].rearrange("p (e c) -> p e c", e=NE)
        qd0 = Qd[0][:, :, :, :].rearrange("p g h t -> p (g h t)")
        rr = [qd0[:, RW * i:RW * i + RW] for i in range(NB)]
        at = RW * NB
        fo = [qd0[:, at + D * i:at + D * i + D] for i in range(NB)]
        at += D * NB
        ft, fx, fxT = ([qd0[:, at + D * (2 * k + i):at + D * (2 * k + i) + D] for i in range(2)] for k in range(3))
        at += 6 * D
        w1s = [qd0[:, at + HID * i:at + HID * i + HID] for i in range(2)]
        at += 2 * HID
        fh = [qd0[:, at + HID * i:at + HID * i + HID].rearrange("p (m t) -> p m t", m=HH) for i in range(2)]
        at += HID * 2
        b1t = [qd0[:, at + HH * i:at + HH * i + HH] for i in range(2)]
        cmpt = Qd[1][:, 0, 0:2, :].rearrange("p a b -> p (a b)")[:, 0:NT * NE].rearrange("p (t e) -> p t e", e=NE)

        oh = (Qd[1][:, 1, 0, :].bitcast(BF16))[:, 0:NU * NE].rearrange("p (u e) -> p u e", e=NE)

        s2p = [pb(f"s2p{i}", [P, 512]) for i in range(2)]
        s1p = [pb(f"s1p{i}", [P, 512]) for i in range(2)]
        pvp = pb("pvp", [P, 512])
        m0 = pb("m0", [P, 512])
        m1 = pb("m1", [P, 512])
        m2 = pb("m2", [P, 512])

        w_in = sem("w_in")
        memset_done = sem("memset_done")
        x_in = [sem(f"x_in{i}") for i in range(2)]
        c_in = [sem(f"c_in{i}") for i in range(2)]
        kd_in = [sem(f"kd_in{i}") for i in range(2)]
        qm_ok = sem("qm_ok")
        qd_v = sem("qd_v")
        qd_a = sem("qd_a")
        setup_v = sem("setup_v")
        setup_a = sem("setup_a")
        setup_p = sem("setup_p")
        setup_t = sem("setup_t")
        stats = sem("stats")
        stat_step = sem("stat_step")
        rstd_ok = sem("rstd_ok")
        pool_step = sem("pool_step")
        xn_ok = sem("xn_ok")
        xb_ok = sem("xb_ok")
        xT_ps = sem("xT_ps")
        cT_ps = sem("cT_ps")
        xT_sb = sem("xT_sb")
        cT_sb = sem("cT_sb")
        q_ps = sem("q_ps")
        k_ps = sem("k_ps")
        v_ps = sem("v_ps")
        q_sb = sem("q_sb")
        k_sb = sem("k_sb")
        qb_ok = sem("qb_ok")
        kb_ok = sem("kb_ok")
        v_sb = sem("v_sb")
        s1_ps = sem("s1_ps")
        mx_ok = sem("mx_ok")
        mT_ps = sem("mT_ps")
        s2_ps = sem("s2_ps")
        pt_ok = sem("pt_ok")
        pv_ps = sem("pv_ps")
        rec_ok = sem("rec_ok")
        ot_ok = sem("ot_ok")
        o_ps = sem("o_ps")
        x1_ok = sem("x1_ok")
        hm_ok = sem("hm_ok")
        fill_ok = sem("fill_ok")
        passed = sem("passed")
        we_in = sem("we_in")
        nrm_ok = sem("nrm_ok")
        wgn_ok = sem("wgn_ok")
        wgT_ok = sem("wgT_ok")
        wc_ok = sem("wc_ok")
        chain = sem("chain")
        pchain = sem("pchain")
        gs1 = sem("gs1")
        g_stat = sem("g_stat")
        g_rstd = sem("g_rstd")
        g_cp = sem("g_cp")
        g_pay = sem("g_pay")
        g_tr = sem("g_tr")
        g_xT = sem("g_xT")
        g_lg = sem("g_lg")
        g_lgv = sem("g_lgv")
        diff_ok = sem("diff_ok")
        ex_ok = sem("ex_ok")
        oh_ok = sem("oh_ok")
        cnt_ps = sem("cnt_ps")
        pos_ok = sem("pos_ok")
        eid_ok = sem("eid_ok")
        gate_ok = sem("gate_ok")
        rec_out = sem("rec_out")
        r_in = [sem(f"r_in{i}") for i in range(NB)]
        f_xn = sem("f_xn")
        f_tr = sem("f_tr")
        f_xT = sem("f_xT")
        f_w = sem("f_w")
        f_h = sem("f_h")
        f_g = sem("f_g")
        f_o = sem("f_o")
        f_t = sem("f_t")
        f_out = sem("f_out")
        scat = [sem(f"scat{i}") for i in range(NB)]
        NW = 5 + 2 * CJ + 3 + 4

        def steps(eng, step):
            def at(s):
                step(s, s % 2, s < NC_, 1 <= s <= NC_, 2 <= s <= NC_ + 1, s >= 3)
            for s in range(4):
                at(s)
            with eng.Fori(2, NC_ // 2 - 1, 1) as i:
                for p in range(2):
                    step(2 * i + p, p, True, True, True, True)
            for s in range(NC_ - 2, NC_ + 3):
                at(s)

        def settle(eng):
            eng.sem_inc(passed, 1)

        def kd_count(s, p):
            return 256 * ((s + 1) // 2) if isinstance(s, int) else 128 * (s + p)

        def tiles(eng, step):
            for k in range(NB):
                step(k, k, min(k, 2), True)
            with eng.Fori(1, NT // NB, 1) as i:
                for q in range(NB):
                    step(NB * i + q, q, 2, True)
            for k in range(NT, NT + 2):
                step(k, k % NB, 3 if k > NT else 2, False)

        block = es.enter_context(nc.Block())

        @block.sync
        def _(sp):
            sp.wait_ge(memset_done, 1)
            sp.dma_start(wq[:, :], W_q).then_inc(w_in, 16)
            sp.dma_start(wk[:, :], W_k).then_inc(w_in, 16)
            sp.dma_start(wv[:, :], W_v).then_inc(w_in, 16)
            for i, b_ in enumerate((b_q, b_k)):
                sp.dma_start(brow[:, i, :, :, 0:DK], b_.rearrange("(o g h d) -> o g h d", o=1, g=G, h=GH)).then_inc(w_in, 16)
            for b in range(2):
                for j in range(CJ):
                    r = 32 * j + HR * b
                    sp.dma_start(wo[r:r + DK, b], W_o.rearrange("(j g d) n -> j d g n", j=CJ, g=4)[j]).then_inc(w_in, 16)
            sp.dma_start(bv[:, :], b_v.rearrange("(o n) -> o n", o=1).to_broadcast([P, D])).then_inc(w_in, 16)
            sp.dma_start(bo[:, :], b_o.rearrange("(o n) -> o n", o=1).to_broadcast([P, D])).then_inc(w_in, 16)
            sp.dma_start(gx[:, :], g_xattn.rearrange("(o n) -> o n", o=1).to_broadcast([P, 1])).then_inc(w_in, 16)
            sp.dma_start(gf[:, :], g_ffn.rearrange("(o n) -> o n", o=1).to_broadcast([P, 1])).then_inc(w_in, 16)
            sp.dma_start(wred[:, :], w_red).then_inc(w_in, 16)
            sp.dma_start(wgs[:, :], wg).then_inc(w_in, 16)
            sp.dma_start(b1s[:, :], b1.rearrange("e (m p) -> (e m) p", m=HH)).then_inc(w_in, 16)
            for c in range(2):
                sp.dma_start(XC[c][:, :, :], x_t[:, CU * c:CU * c + CU]).then_inc(x_in[c], 16)
                sp.dma_start(C[c][:, :, :], c_t[:, CU * c:CU * c + CU]).then_inc(c_in[c], 16)

            def step(s, p, proj, peak, attend, gate):
                if not isinstance(s, int) or s + 2 < NC_:
                    sp.wait_ge(cT_ps, s + 1)
                    cu = bass.ds(CU * (s + 2), CU)
                    sp.dma_start(C[p][:, :, :], c_t[:, cu]).then_inc(c_in[p], 16)
                if proj:
                    if isinstance(s, int) and s == 0:
                        sp.wait_ge(memset_done, 2)
                    if not isinstance(s, int) or s >= 2:
                        sp.wait_ge(s1_ps, 2 * CU * (s - 1))
                    sp.wait_ge(kb_ok, 2 * s + 2)
                    for g in range(G):
                        for h in range(GH):
                            r = slice(HR * h, HR * h + DK)
                            sp.dma_start(Kd[p][r, g, h, :], kb[r, g, :]).then_inc(kd_in[p], 16)
                if not isinstance(s, int) or s + 2 < NC_:
                    if gate:
                        sp.wait_ge(g_tr, s - 2)
                    else:
                        sp.wait_ge(xb_ok, s + 1)
                    sp.dma_start(XC[p][:, :, :], x_t[:, cu]).then_inc(x_in[p], 16)
            steps(sp, step)
            sp.wait_ge(s1_ps, 2 * NU)
            sp.dma_start(w1[:, :, :], W1.rearrange("e c h -> c e h")).then_inc(we_in, 16)
            for e in range(NE):
                sp.dma_start(w2[:, e], W2.rearrange("e (m p) c -> e p m c", m=HH)[e]).then_inc(we_in, 16)
            sp.dma_start(kd1[:, 0:NE * D],
                         b2.rearrange("(o e) c -> o (e c)", o=1).to_broadcast([P, NE * D])).then_inc(we_in, 16)
            sp.wait_ge(rec_out, 16 * NU)
            sp.wait_ge(g_lgv, NC_)

            def load(i, q):
                if not isinstance(i, int):
                    sp.wait_ge(scat[q], (i - q) * (16 // NB))
                sp.dma_start(rr[q], records[bass.ds(P * i, P), :]).then_inc(r_in[q], 16)
            for q in range(NB):
                load(q, q)
            with sp.Fori(1, NT // NB, 1) as k:
                for q in range(NB):
                    load(NB * k + q, q)
            for q in range(NB):
                sp.wait_ge(scat[q], 16 * (NT // NB))

        @block.gpsimd
        def _(pool):
            nc.gpsimd.memset(brow[:, :, :, :, :], 0.0).then_inc(pool_step, 1)
            nc.gpsimd.memset(one[:, :], 1.0)
            nc.gpsimd.memset(mhalf[:, :], -0.5)
            nc.gpsimd.memset(wo[:, :, :, :], 0.0)
            pool.wait_ge(pool_step, 1)
            nc.gpsimd.memset(brow[:, 1, :, :, DK:DK + 1], 1.0).then_inc(memset_done, 1)
            nc.gpsimd.memset(ident[:, :], 0.0).then_inc(pool_step, 1)
            pool.wait_ge(pool_step, 2)
            nc.gpsimd.affine_select(out=ident[:, :], in_=ident[:, :], compare_op=ALU.not_equal, fill=1.0, base=0,
                                    pattern=[[-1, P]], channel_multiplier=1).then_inc(setup_p, 1)
            nc.gpsimd.memset(V[0][:, :, :, :], 0.0)
            nc.gpsimd.memset(V[1][:, :, :, :], 0.0).then_inc(setup_p, 1)
            nc.gpsimd.memset(mx[:, :, :, :, :], 0.0)
            nc.gpsimd.memset(Kd[0][:, :, :, :].bitcast(U32), 0)
            nc.gpsimd.memset(Kd[1][:, :, :, :].bitcast(U32), 0).then_inc(memset_done, 1)
            nc.gpsimd.memset(hmask[:, :], 1.0).then_inc(hm_ok, 1)
            pool.wait_ge(hm_ok, 1)
            nc.gpsimd.affine_select(out=hmask[:, :], in_=hmask[:, :], compare_op=ALU.is_ge, fill=0.0, base=0,
                                    pattern=[[-HR, GH]], channel_multiplier=1).then_inc(hm_ok, 1)
            pool.wait_ge(hm_ok, 2)
            nc.gpsimd.affine_select(out=hmask[:, :], in_=hmask[:, :], compare_op=ALU.is_ge, fill=0.0, base=HR - 1,
                                    pattern=[[HR, GH]], channel_multiplier=-1).then_inc(hm_ok, 1)
            nc.gpsimd.memset(tri[:, :], 1.0)
            nc.gpsimd.memset(ones[:, :], 1.0)
            nc.gpsimd.memset(blank[:, :], 0.0)
            for e in range(NE):
                nc.gpsimd.memset(rank[:, e:e + 1], float(NE - e))
            nc.gpsimd.iota(tile_i[:, :], pattern=[[1, NT]], base=0, channel_multiplier=0)
            nc.gpsimd.iota(token[:, :], pattern=[[P, NU]], base=0, channel_multiplier=1).then_inc(pchain, 1)
            pool.wait_ge(pchain, 1)
            nc.gpsimd.affine_select(out=tri[:, :], in_=tri[:, :], compare_op=ALU.is_gt, fill=0.0, base=0,
                                    pattern=[[1, P]], channel_multiplier=-1)
            nc.gpsimd.tensor_copy(tile_no[:, :], tile_i[:, :])
            nc.gpsimd.tensor_copy(XR[:, :, R_ID].bitcast(I32), token[:, :])
            nc.gpsimd.memset(blank[:, R_ID:R_ID + 1].bitcast(I32), N).then_inc(pchain, 1)
            pool.wait_ge(pchain, 2)
            pool.dma_start(records.rearrange("(t p) w -> p t w", p=P),
                           blank[:, :].rearrange("p (o w) -> p o w", o=1).to_broadcast([P, NT, RW])).then_inc(fill_ok, 16)
            pool.wait_ge(nrm_ok, 1)
            nc.gpsimd.tensor_tensor(nrm[:, 1:2], nrm[:, 0:1], nrm[:, 3:4], ALU.pow).then_inc(nrm_ok, 1)
            pool.wait_ge(setup_a, 1)
            pool.wait_ge(w_in, 16 * NW)
            nc.gpsimd.tensor_scalar(tgbo[:, :], bo[:, :], tg[:, 0:1], None, ALU.mult).then_inc(pool_step, 1)
            pool.wait_ge(pool_step, 3)

            def norm(c, p):
                pool.wait_ge(stats, c + 1)
                nc.gpsimd.tensor_tensor(rstd[:, :], ve[:, :], mhalf[:, :], ALU.pow).then_inc(rstd_ok, 1)
                pool.wait_ge(rstd_ok, c + 1)
                if not isinstance(c, int) or c >= 1:
                    pool.wait_ge(xT_ps, c)
                settle(pool)
                for u in range(CU):
                    i = nc.gpsimd.tensor_scalar(xn[:, u, :], XC[p][:, u, :],
                                                mv[:, u, 0:1], rstd[:, u:u + 1], ALU.subtract, ALU.mult)
                i.then_inc(xn_ok, 1)
                for u in range(CU):
                    i = nc.gpsimd.tensor_tensor(X[:, bass.ds(CU * c + u, 1), :].rearrange("p o d -> p (o d)"),
                                                XC[p][:, u, :], tgbo[:, :], ALU.add)
                i.then_inc(xb_ok, 1)

            norm(0, 0)

            def gate_norm(c):
                pool.wait_ge(g_stat, c + 1)
                nc.gpsimd.tensor_tensor(grstd[:, :], gve[:, :], mhalf[:, :], ALU.pow).then_inc(g_rstd, 1)
                pool.wait_ge(g_rstd, c + 1)
                settle(pool)
                nc.gpsimd.tensor_copy(XR[:, bass.ds(CU * c, CU), R_MEAN], gmv[:, :, 0])
                nc.gpsimd.tensor_copy(XR[:, bass.ds(CU * c, CU), R_RSTD], grstd[:, :]).then_inc(g_pay, 1)

            def step(s, p, proj, peak, attend, gate):
                if gate:
                    if proj:
                        pool.wait_ge(xb_ok, s + 1)
                    else:
                        pool.wait_ge(g_tr, s - 4)
                    pool.wait_ge(x1_ok, CU * (s - 2))
                    settle(pool)
                    nc.gpsimd.tensor_copy(XC[p][:, :, :], X[:, bass.ds(CU * (s - 3), CU), :]).then_inc(g_cp, 1)
                    gate_norm(s - 3)
                if proj and (not isinstance(s, int) or s + 1 < NC_):
                    norm(s + 1, 1 - p)
            steps(pool, step)

            pool.wait_ge(fill_ok, 16)
            pool.wait_ge(pos_ok, 1)
            pool.wait_ge(gate_ok, 1)
            for u in range(NU):
                nc.gpsimd.indirect_dma_start(out=records, out_offset=bass.IndirectOffsetOnAxis(ap=pos[:, u:u + 1], axis=0),
                                             in_=XR[:, u, :], in_offset=None).then_inc(rec_out, 16)

            def scatter(i, q):
                pool.wait_ge(f_out, i + 1)
                settle(pool)
                nc.gpsimd.indirect_dma_start(
                    out=out_rows, out_offset=bass.IndirectOffsetOnAxis(ap=rr[q][:, R_ID:R_ID + 1].bitcast(U32), axis=0),
                    in_=fo[q], in_offset=None, bounds_check=N - 1, oob_is_err=False).then_inc(scat[q], 16)
            def tstep(k, q, head, tail):
                if head >= 2:
                    scatter(k - 2, (q + NB - 2) % NB)
            tiles(pool, tstep)

        @block.scalar
        def _(act):
            act.wait_ge(w_in, 16 * NW)
            nc.scalar.activation(tg[:, :], gx[:, :], ACT.Tanh).then_inc(setup_a, 1)
            act.wait_ge(setup_t, 1)
            nc.scalar.mul(b16[:, 0, :], m0[:, 0:G], ISC).then_inc(setup_a, 1)
            nc.scalar.activation(b16[:, 1, :], m0[:, G:2 * G], ACT.Copy).then_inc(setup_a, 1)
            act.wait_ge(setup_a, 3)
            nc.scalar.activation(tgf[:, :], gf[:, :], ACT.Tanh).then_inc(setup_a, 1)

            def exp(s, u):
                c = s - 2
                for g in range(G):
                    act.wait_ge(s2_ps, 2 * CU * c + 2 * u + g + 1)
                    if u < 2:
                        if not isinstance(s, int) or s >= 3:
                            act.wait_ge(pv_ps, CU * c + u - 1)
                    else:
                        act.wait_ge(pv_ps, CU * c + u - 1)
                    nc.scalar.activation(PT[u % 2][:, GH * g:GH * g + GH, :], s2p[g][:, :].rearrange("p (h q) -> p h q", h=GH),
                                         ACT.Exp).then_inc(pt_ok, 1)

            def step(s, p, proj, peak, attend, gate):
                if proj:
                    act.wait_ge(xT_ps, s + 1)
                    nc.scalar.activation(xT[:, :], m0[:, :], ACT.Copy).then_inc(xT_sb, 1)
                    act.wait_ge(cT_ps, s + 1)
                    if not isinstance(s, int) or s >= 4:
                        act.wait_ge(g_lg, s - 3)
                    nc.scalar.activation(cT[:, :], m1[:, :], ACT.Copy).then_inc(cT_sb, 1)
                if attend:
                    exp(s, 0)
                if proj:
                    if not isinstance(s, int) or s >= 1:
                        act.wait_ge(kd_in[1 - p], kd_count(s, p))
                    for g, m in enumerate((m0, m1)):
                        act.wait_ge(k_ps, 2 * s + g + 1)
                        nc.scalar.activation(kb[:, g, :], m[:, :], ACT.Identity, bias=b16[:, 1, g:g + 1]).then_inc(kb_ok, 1)
                if attend:
                    for u in range(1, CU):
                        exp(s, u)
                if proj:
                    for g, m in enumerate((m0, m1)):
                        nc.scalar.activation(kT[p][:, g, :], m[:, :], ACT.Identity, bias=b16[:, 1, g:g + 1]).then_inc(k_sb, 1)
                if gate:
                    act.wait_ge(g_tr, s - 2)
                    nc.scalar.activation(cT[:, :], m1[:, :], ACT.Copy).then_inc(g_xT, 1)
                if peak:
                    if isinstance(s, int) and s == 1:
                        act.wait_ge(hm_ok, 3)
                    act.wait_ge(qm_ok, 2 * s)
                    for h in range(GH):
                        a = nc.scalar.activation(Qd[1 - p][:, 1, h, :], Q16[1 - p][:, 1, :], ACT.Copy, scale=hmask[:, h:h + 1])
                    a.then_inc(qd_a, 1)
                if proj:
                    for g, m in enumerate(s1p):
                        act.wait_ge(q_ps, 2 * s + g + 1)
                        nc.scalar.activation(qb[:, g, :], m[:, :], ACT.Identity, bias=b16[:, 0, g:g + 1],
                                             scale=ISC).then_inc(qb_ok, 1)
                    for g, m in enumerate(s1p):
                        nc.scalar.activation(Q16[p][:, g, :], m[:, :], ACT.Identity, bias=b16[:, 0, g:g + 1],
                                             scale=ISC).then_inc(q_sb, 1)
            steps(act, step)

            act.wait_ge(diff_ok, 1)
            nc.scalar.activation(ex, lg[:, :, :], ACT.Exp).then_inc(ex_ok, 1)

            act.wait_ge(eid_ok, 1)
            act.wait_ge(we_in, 16 * (2 + NE))

            def stage(k, q):
                p = q % 2
                e = act.value_load(eid[0:1, bass.ds(k, 1)], min_val=0, max_val=NE - 1)
                if not isinstance(k, int) or k >= 2:
                    act.wait_ge(f_g, k - 1)
                nc.scalar.activation(w1s[p], w1[:, bass.ds(e, 1), :].rearrange("p o h -> p (o h)"), ACT.Copy)
                nc.scalar.activation(b1t[p], b1c[:, bass.ds(e, 1), :].rearrange("p o m -> p (o m)"), ACT.Copy).then_inc(f_w, 1)

            def tstep(k, q, head, tail):
                if tail:
                    stage(k, q)
                if head >= 1 and (tail or k == NT):
                    i, p = k - 1, 1 - q % 2
                    act.wait_ge(f_w, i + 1)
                    act.wait_ge(f_h, i + 1)
                    if not isinstance(i, int) or i >= 2:
                        act.wait_ge(f_o, i - 1)
                    for m in range(HH):
                        a = nc.scalar.activation(fh[p][:, m, :], s1p[p][:, P * m:P * m + P], ACT.Gelu, bias=b1t[p][:, m:m + 1])
                    a.then_inc(f_g, 1)
            tiles(act, tstep)

        @block.vector
        def _(dve):
            nc.vector.memset(ksum[:, :], 0.0).then_inc(setup_v, 1)
            dve.wait_ge(setup_v, 1)
            nc.vector.memset(ksum[0:S, 0:HR], 1.0)
            nc.vector.memset(ksum[S:P, HR:2 * HR], 1.0)
            nc.vector.memset(w16[:, :, :, :, :], 0.0).then_inc(setup_v, 1)
            dve.wait_ge(setup_v, 2)
            dve.wait_ge(w_in, 16 * NW)
            nc.vector.tensor_copy(w16[:, 0, :, :, 0:DK], wq[:, :].rearrange("p (g h d) -> p g h d", g=G, h=GH))
            nc.vector.tensor_copy(w16[:, 1, :, :, 0:DK], wk[:, :].rearrange("p (g h d) -> p g h d", g=G, h=GH)).then_inc(setup_v, 1)

            def stat(c, p):
                dve.wait_ge(x_in[p], 16 * (c // 2) + 16 if isinstance(c, int) else 8 * (c - p) + 16)
                if not isinstance(c, int) or c >= 1:
                    dve.wait_ge(xn_ok, c)
                for u in range(CU):
                    i = nc.vector.bn_stats(st[:, u, :], XC[p][:, u, :])
                i.then_inc(stat_step, 1)
                dve.wait_ge(stat_step, 2 * c + 1)
                settle(dve)
                for u in range(CU):
                    i = nc.vector.bn_aggr(mv[:, u, :], st[:, u, :])
                i.then_inc(stat_step, 1)
                dve.wait_ge(stat_step, 2 * c + 2)
                nc.vector.tensor_scalar_add(ve[:, :], mv[:, :, 1], EPS).then_inc(stats, 1)

            def peak_of(s, u):
                for g in range(G):
                    dve.wait_ge(s1_ps, 2 * CU * (s - 1) + 2 * u + g + 1)
                    if u == 0 and g == 0 and (not isinstance(s, int) or s >= 2):
                        dve.wait_ge(mT_ps, 2 * s - 2)
                    nc.vector.tensor_reduce(mx[:, u, g, :, DK], s1p[g][:, :].rearrange("p (h k) -> p h k", h=GH),
                                            AX_X, ALU.max).then_inc(mx_ok, 1)

            def norm_of(s, u):
                n = CU * (s - 2) + u
                dve.wait_ge(pv_ps, n + 1)
                nc.vector.reciprocal(rec[:, :], pvp[:, CJ * S:2 * CJ * S]).then_inc(rec_ok, 1)
                dve.wait_ge(rec_ok, n + 1)
                if u >= 2 or not isinstance(s, int) or s >= 3:
                    dve.wait_ge(o_ps, n - 1)
                nc.vector.tensor_tensor(OT[u % 2][:, :, :].rearrange("p g q -> p (g q)"), pvp[:, 0:CJ * S], rec[:, :],
                                        ALU.mult).then_inc(ot_ok, 1)

            def x1_of(s, u):
                n = CU * (s - 2) + u
                dve.wait_ge(o_ps, n + 1)
                dve.wait_ge(xb_ok, s - 1)
                xu = X[:, bass.ds(n, 1), :].rearrange("p o d -> p (o d)")
                nc.vector.scalar_tensor_tensor(out=xu, in0=m2[:, 0:D], scalar=tg[:, 0:1], in1=xu,
                                               op0=ALU.mult, op1=ALU.add).then_inc(x1_ok, 1)

            vc = [0]

            def link(i):
                vc[0] += 1
                i.then_inc(chain, 1)
                dve.wait_ge(chain, vc[0])

            nc.vector.memset(nrm[:, 3:4], 0.5)
            link(nc.vector.tensor_tensor(wg2[:, :], wgs[:, :], wgs[:, :], ALU.mult))
            nc.vector.tensor_reduce(nrm[:, 0:1], wg2[:, :], AX_X, ALU.add).then_inc(nrm_ok, 1)
            dve.wait_ge(nrm_ok, 2)
            link(nc.vector.tensor_scalar_max(nrm[:, 2:3], nrm[:, 1:2], 1e-4))
            link(nc.vector.reciprocal(nrm[:, 0:1], nrm[:, 2:3]))
            nc.vector.tensor_scalar(wgn[:, :], wgs[:, :], nrm[:, 0:1], None, ALU.mult).then_inc(wgn_ok, 1)
            dve.wait_ge(setup_t, 2)
            nc.vector.tensor_copy(b1c[:, :, :].rearrange("p e m -> p (e m)"), s1p[0][:, 0:NE * HH])
            link(nc.vector.tensor_copy(wredT[:, :], m1[0:GD, 0:P]))
            link(nc.vector.tensor_reduce(wmean[:, 0:1], wredT[:, :], AX_X, ALU.add))
            link(nc.vector.tensor_scalar_mul(wmean[:, 1:2], wmean[:, 0:1], 1.0 / D))
            nc.vector.tensor_scalar(wredT[:, :], wredT[:, :], wmean[:, 1:2], None, ALU.subtract).then_inc(wgT_ok, 1)
            dve.wait_ge(setup_t, 3)
            nc.vector.tensor_copy(wgT[:, :], m2[0:GD, 0:NE]).then_inc(wgT_ok, 1)
            dve.wait_ge(setup_t, 4)
            nc.vector.tensor_copy(wc[:, :], pvp[:, 0:NE]).then_inc(wc_ok, 1)

            def gate_stat(c):
                dve.wait_ge(x1_ok, CU * c + CU)
                if not isinstance(c, int) or c >= 1:
                    dve.wait_ge(g_pay, c)
                settle(dve)
                for u in range(CU):
                    i = nc.vector.bn_stats(gst[:, u, :], X[:, bass.ds(CU * c + u, 1), :].rearrange("p o d -> p (o d)"))
                i.then_inc(gs1, 1)
                dve.wait_ge(gs1, 2 * c + 1)
                settle(dve)
                for u in range(CU):
                    i = nc.vector.bn_aggr(gmv[:, u, :], gst[:, u, :])
                i.then_inc(gs1, 1)
                dve.wait_ge(gs1, 2 * c + 2)
                nc.vector.tensor_scalar_add(gve[:, :], gmv[:, :, 1], EPS).then_inc(g_stat, 1)

            def gate_keep(c):
                dve.wait_ge(g_lg, c + 1)
                dve.wait_ge(g_pay, c + 1)
                cu = bass.ds(CU * c, CU)
                nc.vector.tensor_tensor(lg[:, cu, :], pvp[:, 0:CU * NE].rearrange("p (u e) -> p u e", e=NE),
                                        XR[:, cu, R_RSTD:R_RSTD + 1].to_broadcast([P, CU, NE]), ALU.mult).then_inc(g_lgv, 1)

            stat(0, 0)

            def step(s, p, proj, peak, attend, gate):
                if peak:
                    peak_of(s, 0)
                if gate:
                    gate_stat(s - 3)
                if peak:
                    peak_of(s, 1)
                if attend:
                    norm_of(s, 0)
                if peak:
                    peak_of(s, 2)
                if attend:
                    norm_of(s, 1)
                    x1_of(s, 0)
                if peak:
                    peak_of(s, 3)
                if proj and (not isinstance(s, int) or s + 1 < NC_):
                    stat(s + 1, 1 - p)
                if attend:
                    norm_of(s, 2)
                    x1_of(s, 1)
                if peak:
                    for g, m in enumerate(s1p):
                        dve.wait_ge(mT_ps, 2 * (s - 1) + g + 1)
                        nc.vector.tensor_tensor(Q16[1 - p][:, g, :], Q16[1 - p][:, g, :], m[:, :],
                                                ALU.subtract).then_inc(qm_ok, 1)
                if attend:
                    norm_of(s, 3)
                if proj:
                    dve.wait_ge(v_ps, s + 1)
                    if isinstance(s, int) and s < 2:
                        dve.wait_ge(setup_p, 2)
                    for b in range(2):
                        r = slice(S * b, S * b + S)
                        i = nc.vector.tensor_tensor(
                            V[p][r, :, :, HR * b:HR * b + DK],
                            m0[r, :].rearrange("p (u h d) -> p u h d", u=CU, h=H),
                            bv[r, :].rearrange("p (o h d) -> p o h d", o=1, h=H).to_broadcast([S, CU, H, DK]), ALU.add)
                    i.then_inc(v_sb, 1)
                if attend:
                    x1_of(s, 2)
                if peak:
                    dve.wait_ge(qm_ok, 2 * s - 1)
                    if isinstance(s, int) and s == 1:
                        dve.wait_ge(hm_ok, 3)
                    for h in range(GH):
                        i = nc.vector.tensor_scalar(Qd[1 - p][:, 0, h, :], Q16[1 - p][:, 0, :], hmask[:, h:h + 1], None, ALU.mult)
                    i.then_inc(qd_v, 1)
                if attend:
                    x1_of(s, 3)
                if gate:
                    gate_keep(s - 3)
            steps(dve, step)

            dve.wait_ge(g_lgv, NC_)

            def col(a, n=1):
                return small[:, a * NU:a * NU + n * NU]

            def wide(ap):
                return ap.rearrange("p (u o) -> p u o", o=1).to_broadcast([P, NU, NE])

            def per_expert(ap):
                return ap.rearrange("p (o e) -> p o e", o=1).to_broadcast([P, NU, NE])

            link(nc.vector.tensor_reduce(col(0), lg[:, :, :], AX_X, ALU.max))
            nc.vector.tensor_tensor(lg[:, :, :], lg[:, :, :], wide(col(0)), ALU.subtract).then_inc(diff_ok, 1)
            dve.wait_ge(ex_ok, 1)
            nc.vector.tensor_reduce(col(1), ex, AX_X, ALU.add)
            link(nc.vector.tensor_reduce(col(2), ex, AX_X, ALU.max))
            link(nc.vector.reciprocal(col(3), col(1)))
            link(nc.vector.tensor_tensor(col(4), col(2), col(3), ALU.mult))
            dve.wait_ge(setup_a, 4)
            nc.vector.tensor_scalar(XR[:, :, R_GATE], col(4), tgf[:, 0:1], None, ALU.mult).then_inc(gate_ok, 1)
            link(nc.vector.tensor_tensor(ky, ex, wide(col(2)), ALU.is_equal))
            link(nc.vector.tensor_tensor(ky, ky, per_expert(rank[:, :]), ALU.mult))
            link(nc.vector.tensor_reduce(col(5), ky, AX_X, ALU.max))
            nc.vector.tensor_tensor(oh[:, :, :], ky, wide(col(5)), ALU.is_equal).then_inc(oh_ok, 1)
            dve.wait_ge(cnt_ps, 2)
            nc.vector.tensor_copy(tot, m1[:, :].rearrange("p (u e) -> p u e", e=NE))
            link(nc.vector.tensor_copy(ta, m1[:, :].rearrange("p (u e) -> p u e", e=NE)))
            a, b, k = ta, tb, 1
            while k < NU:
                nc.vector.tensor_copy(b[:, 0:k, :], a[:, 0:k, :])
                link(nc.vector.tensor_tensor(b[:, k:NU, :], a[:, k:NU, :], a[:, 0:NU - k, :], ALU.add))
                a, b, k = b, a, 2 * k
            tl = lambda n: col(6 + n)[:, 0:NE]
            link(nc.vector.tensor_scalar_add(tl(0).bitcast(I32), a[:, NU - 1, :], float(P - 1)))
            link(nc.vector.tensor_single_scalar(tl(1).bitcast(I32), tl(0).bitcast(I32), 7, ALU.arith_shift_right))
            nc.vector.tensor_copy(tl(2), tl(1).bitcast(I32))
            link(nc.vector.tensor_copy(tl(3), tl(1).bitcast(I32)))
            c, d, k = 3, 4, 1
            while k < NE:
                nc.vector.tensor_copy(tl(d)[:, 0:k], tl(c)[:, 0:k])
                link(nc.vector.tensor_tensor(tl(d)[:, k:NE], tl(c)[:, k:NE], tl(c)[:, 0:NE - k], ALU.add))
                c, d, k = d, c, 2 * k
            link(nc.vector.tensor_tensor(tl(5), tl(c), tl(2), ALU.subtract))
            link(nc.vector.tensor_scalar_mul(tl(5), tl(5), float(P)))
            link(nc.vector.tensor_tensor(b, a, tot, ALU.subtract))
            link(nc.vector.tensor_tensor(b, b, per_expert(tl(5)), ALU.add))
            link(nc.vector.tensor_tensor(b, m0[:, :].rearrange("p (u e) -> p u e", e=NE), b, ALU.add))
            link(nc.vector.tensor_tensor(b, b, oh[:, :, :], ALU.mult))
            link(nc.vector.tensor_reduce(col(1), b, AX_X, ALU.add))
            nc.vector.tensor_copy(pos[:, :], col(1)).then_inc(pos_ok, 1)
            link(nc.vector.tensor_tensor(
                cmpt, tl(c).rearrange("p (o e) -> p o e", o=1).to_broadcast([P, NT, NE]),
                tile_no[:, :].rearrange("p (t o) -> p t o", o=1).to_broadcast([P, NT, NE]), ALU.is_le))
            cnt = Qd[1][:, 0, 2, 0:NT]
            link(nc.vector.tensor_reduce(cnt, cmpt, AX_X, ALU.add))
            nc.vector.tensor_scalar_min(eid[:, :], cnt, float(NE - 1)).then_inc(eid_ok, 1)
            dve.wait_ge(eid_ok, 1)
            dve.wait_ge(we_in, 16 * (2 + NE))

            def ft_norm(i, q):
                p = q % 2
                if isinstance(i, int):
                    dve.wait_ge(r_in[q], 16 * (i // NB) + 16)
                else:
                    dve.wait_ge(r_in[q], (i - q) * (16 // NB) + 16)
                if not isinstance(i, int) or i >= 2:
                    dve.wait_ge(f_tr, i - 1)
                nc.vector.tensor_scalar(fx[p], rr[q][:, 0:D], rr[q][:, R_MEAN:R_MEAN + 1], rr[q][:, R_RSTD:R_RSTD + 1],
                                        ALU.subtract, ALU.mult).then_inc(f_xn, 1)

            def ft_copy(i, q):
                p = q % 2
                dve.wait_ge(f_tr, i + 1)
                if not isinstance(i, int) or i >= 2:
                    dve.wait_ge(f_h, i - 1)
                nc.vector.tensor_copy(fxT[p], s2p[p][:, 0:P]).then_inc(f_xT, 1)

            def ft_out(i, q):
                p = q % 2
                e = dve.value_load(eid[0:1, bass.ds(i, 1)], min_val=0, max_val=NE - 1)
                dve.wait_ge(f_o, i + 1)
                nc.vector.tensor_tensor(ft[p], (m0, m1)[p][:, 0:D], b2r[:, bass.ds(e, 1), :].rearrange("p o c -> p (o c)"),
                                        ALU.add).then_inc(f_t, 1)
                dve.wait_ge(f_t, i + 1)
                if not isinstance(i, int) or i >= NB:
                    dve.wait_ge(scat[q], (i - q) * (16 // NB))
                nc.vector.scalar_tensor_tensor(out=fo[q], in0=ft[p], scalar=rr[q][:, R_GATE:R_GATE + 1],
                                               in1=rr[q][:, 0:D], op0=ALU.mult, op1=ALU.add).then_inc(f_out, 1)

            ft_norm(0, 0)

            for k in range(NB):
                ft_norm(k + 1, (k + 1) % NB)
                ft_copy(k, k)
                if k >= 2:
                    ft_out(k - 2, k - 2)
            with dve.Fori(1, NT // NB - 1, 1) as i:
                for q in range(NB):
                    ft_norm(NB * i + q + 1, (q + 1) % NB)
                    ft_copy(NB * i + q, q)
                    ft_out(NB * i + q - 2, (q + NB - 2) % NB)
            for k in range(NT - NB, NT + 2):
                if k + 1 < NT:
                    ft_norm(k + 1, (k + 1) % NB)
                if k < NT:
                    ft_copy(k, k % NB)
                ft_out(k - 2, (k - 2) % NB)

        @block.tensor
        def _(pe):
            pe.wait_ge(setup_p, 1)
            pe.wait_ge(w_in, 16 * NW)
            for g in range(2 * G):
                i = nc.tensor.matmul(m0[:, g:g + 1], brow[0:1, g // G, g % G].rearrange("p h r -> p (h r)"), one[0:1, 0:1],
                                     start=(g == 0), stop=True, skip_group_check=True)
            i.then_inc(setup_t, 1)
            nc.tensor.transpose(s1p[0][:, 0:NE * HH], b1s[:, :], ident[0:NE * HH, 0:NE * HH])
            nc.tensor.transpose(m1[0:GD, 0:P], wred[:, :], ident[:, :]).then_inc(setup_t, 1)
            pe.wait_ge(wgn_ok, 1)
            nc.tensor.transpose(m2[0:GD, 0:NE], wgn[:, :], ident[0:NE, 0:NE]).then_inc(setup_t, 1)
            pe.wait_ge(wgT_ok, 2)
            nc.tensor.matmul(pvp[:, 0:NE], wredT[:, :], wgT[:, :], start=True, stop=True).then_inc(setup_t, 1)
            pe.wait_ge(wc_ok, 1)
            pe.wait_ge(setup_a, 3)
            pe.wait_ge(setup_v, 3)

            def scores2(s, u, p):
                for g in range(G):
                    n = 2 * CU * (s - 2) + 2 * u + g
                    if u or not isinstance(s, int) or s >= 3:
                        pe.wait_ge(pt_ok, n - 1)
                    if u == 0:
                        pe.wait_ge(qd_a if g else qd_v, s - 1)
                    for b in range(2):
                        t = slice(UNIT * u + S * b, UNIT * u + S * b + S)
                        i = nc.tensor.matmul(s2p[g][S * b:S * b + S, :].rearrange("p (h q) -> p h q", h=GH),
                                             kT[p][:, g, t], Qd[p][:, g, :, t], start=True, stop=True)
                    i.then_inc(s2_ps, 1)

            def scores1(s, u, p):
                for g in range(G):
                    n = 2 * CU * (s - 1) + 2 * u + g
                    if u or not isinstance(s, int) or s >= 2:
                        pe.wait_ge(mx_ok, n - 1)
                    for b in range(2):
                        t = slice(UNIT * u + S * b, UNIT * u + S * b + S)
                        i = nc.tensor.matmul(s1p[g][S * b:S * b + S, :].rearrange("p (h q) -> p h q", h=GH),
                                             qb[:, g, t], Kd[p][:, g, :, t], start=True, stop=True)
                    i.then_inc(s1_ps, 1)

            def values(s, u, p):
                n = CU * (s - 2) + u
                pe.wait_ge(pt_ok, 2 * n + 2)
                if u == 0:
                    pe.wait_ge(v_sb, s - 1)
                    if not isinstance(s, int) or s >= 4:
                        pe.wait_ge(g_lgv, s - 3)
                if u or not isinstance(s, int) or s >= 3:
                    pe.wait_ge(ot_ok, n)
                for j in range(CJ):
                    nc.tensor.matmul(pvp[32 * j:32 * j + 32, CJ * S:2 * CJ * S], ksum[:, :],
                                     PT[u % 2][:, 4 * j:4 * j + 4, :].rearrange("p h q -> p (h q)"),
                                     start=True, stop=False, skip_group_check=True)
                for g in range(4):
                    for j in range(CJ):
                        i = nc.tensor.matmul(pvp[32 * j:32 * j + 32, S * g:S * g + S], V[p][:, u, 4 * j + g, :],
                                             PT[u % 2][:, 4 * j + g, :], start=False, stop=(g == 3), skip_group_check=True)
                i.then_inc(pv_ps, 1)

            def project_out(s, u):
                n = CU * (s - 2) + u
                pe.wait_ge(ot_ok, n + 1)
                if u or not isinstance(s, int) or s > 2:
                    pe.wait_ge(x1_ok, n)
                for g in range(4):
                    for b in range(2):
                        i = nc.tensor.matmul(m2[S * b:S * b + S, 0:D], OT[u % 2][:, g, :], wo[:, b, g, :],
                                             start=(g == 0), stop=(g == 3), skip_group_check=True)
                i.then_inc(o_ps, 1)

            def step(s, p, proj, peak, attend, gate):
                if proj:
                    pe.wait_ge(xn_ok, s + 1)
                    if not isinstance(s, int) or s >= 1:
                        pe.wait_ge(v_sb, s)
                    for u in range(CU):
                        i = nc.tensor.transpose(m0[:, UNIT * u:UNIT * u + UNIT], xn[:, u, :], ident[:, :])
                    i.then_inc(xT_ps, 1)
                    pe.wait_ge(c_in[p], 16 * (s // 2) + 16 if isinstance(s, int) else 8 * (s - p) + 16)
                    for u in range(CU):
                        i = nc.tensor.transpose(m1[:, UNIT * u:UNIT * u + UNIT], C[p][:, u, :], ident[:, :])
                    i.then_inc(cT_ps, 1)
                if peak:
                    pe.wait_ge(qb_ok, 2 * s)
                    pe.wait_ge(q_sb, 2 * s)
                    pe.wait_ge(kd_in[1 - p], kd_count(s, p))
                    scores1(s, 0, 1 - p)
                if attend:
                    scores2(s, 0, p)
                if peak:
                    scores1(s, 1, 1 - p)
                if proj:
                    pe.wait_ge(xT_sb, s + 1)
                    pe.wait_ge(cT_sb, s + 1)
                    for g, m in enumerate((m0, m1)):
                        nc.tensor.matmul(m[:, :], w16[:, 1, g].rearrange("p h r -> p (h r)"), cT[:, :], start=True,
                                         stop=True).then_inc(k_ps, 1)
                if attend:
                    scores2(s, 1, p)
                    values(s, 0, p)
                if peak:
                    scores1(s, 2, 1 - p)
                if attend:
                    scores2(s, 2, p)
                    values(s, 1, p)
                    project_out(s, 0)
                    scores2(s, 3, p)
                if peak:
                    scores1(s, 3, 1 - p)
                if attend:
                    values(s, 2, p)
                if proj:
                    pe.wait_ge(k_sb, 2 * s + 2)
                    for u in range(CU):
                        i = nc.tensor.matmul(m0[:, D * u:D * u + D], cT[:, UNIT * u:UNIT * u + UNIT], wv[:, :],
                                             start=(u == 0), stop=(u == CU - 1), skip_group_check=True)
                    i.then_inc(v_ps, 1)
                if gate:
                    pe.wait_ge(g_cp, s - 2)
                    for u in range(CU):
                        i = nc.tensor.transpose(m1[:, UNIT * u:UNIT * u + UNIT], XC[p][:, u, :], ident[:, :])
                    i.then_inc(g_tr, 1)
                if attend:
                    project_out(s, 1)
                if peak:
                    pe.wait_ge(mx_ok, 2 * CU * s)
                    for g, m in enumerate(s1p):
                        for u in range(CU):
                            i = nc.tensor.transpose(m[:, UNIT * u:UNIT * u + UNIT],
                                                    mx[:, u, g].rearrange("p h r -> p (h r)"), ident[:, :])
                        i.then_inc(mT_ps, 1)
                if attend:
                    values(s, 3, p)
                if proj:
                    for g, m in enumerate(s1p):
                        if peak:
                            pe.wait_ge(qm_ok, 2 * (s - 1) + g + 1)
                        nc.tensor.matmul(m[:, :], w16[:, 0, g].rearrange("p h r -> p (h r)"), xT[:, :], start=True,
                                         stop=True).then_inc(q_ps, 1)
                if attend:
                    project_out(s, 2)
                    project_out(s, 3)
                if gate:
                    pe.wait_ge(g_xT, s - 2)
                    if attend:
                        pe.wait_ge(ot_ok, CU * (s - 1))
                    else:
                        pe.wait_ge(g_lgv, s - 3)
                    for u in range(CU):
                        i = nc.tensor.matmul(pvp[:, NE * u:NE * u + NE], cT[:, UNIT * u:UNIT * u + UNIT], wc[:, :],
                                             start=True, stop=True, skip_group_check=True)
                    i.then_inc(g_lg, 1)
            steps(pe, step)

            pe.wait_ge(oh_ok, 1)
            nc.tensor.matmul(m0[:, :], tri[:, :], oh[:, :, :].rearrange("p u e -> p (u e)"), start=True, stop=True).then_inc(cnt_ps, 1)
            nc.tensor.matmul(m1[:, :], ones[:, :], oh[:, :, :].rearrange("p u e -> p (u e)"), start=True, stop=True).then_inc(cnt_ps, 1)

            pe.wait_ge(eid_ok, 1)
            pe.wait_ge(we_in, 16 * (2 + NE))
            def tstep(k, q, head, tail):
                p = q % 2
                if tail:
                    pe.wait_ge(f_xn, k + 1)
                    if not isinstance(k, int) or k >= 2:
                        pe.wait_ge(f_xT, k - 1)
                    nc.tensor.transpose(s2p[p][:, 0:P], fx[p], ident[:, :]).then_inc(f_tr, 1)
                if head >= 1 and (tail or k == NT):
                    i, r = k - 1, 1 - p
                    pe.wait_ge(f_xT, i + 1)
                    pe.wait_ge(f_w, i + 1)
                    if not isinstance(i, int) or i >= 2:
                        pe.wait_ge(f_g, i - 1)
                    for m in range(HH):
                        j = nc.tensor.matmul(s1p[r][:, P * m:P * m + P], w1s[r][:, P * m:P * m + P], fxT[r],
                                             start=(m == 0), stop=(m == HH - 1), skip_group_check=True)
                    j.then_inc(f_h, 1)
                if head >= 2:
                    i = k - 2
                    e = pe.value_load(eid[0:1, bass.ds(i, 1)], min_val=0, max_val=NE - 1)
                    pe.wait_ge(f_g, i + 1)
                    if not isinstance(i, int) or i >= 2:
                        pe.wait_ge(f_t, i - 1)
                    for m in range(HH):
                        j = nc.tensor.matmul((m0, m1)[p][:, 0:D], fh[p][:, m, :],
                                             w2[:, bass.ds(e, 1), m, :].rearrange("p o c -> p (o c)"),
                                             start=(m == 0), stop=(m == HH - 1))
                    j.then_inc(f_o, 1)
            tiles(pe, tstep)


_INS = ["x", "ctx_1024", "g_xattn", "g_ffn", "L0_xattn_W_q", "L0_xattn_b_q", "L0_xattn_W_k", "L0_xattn_b_k",
        "L0_xattn_W_v", "L0_xattn_b_v", "L0_xattn_W_o", "L0_xattn_b_o", "L0_ffn_w_red", "L0_ffn_wg",
        "L0_ffn_W1", "L0_ffn_b1", "L0_ffn_W2", "L0_ffn_b2"]


def kernel(**inputs):
    import numpy as _np
    import concourse.bacc as _bacc
    from concourse import mybir as _mybir
    from concourse.bass_utils import run_bass_kernel_spmd as _run

    nc = _bacc.Bacc("TRN2", target_bir_lowering=False, num_devices=1)
    arrays, args = {}, []
    for name in _INS:
        a = _np.ascontiguousarray(inputs[name])
        arrays[f"in_{name}"] = a
        args.append(nc.dram_tensor(f"in_{name}", a.shape, _mybir.dt.from_np(a.dtype), kind="ExternalInput").ap())
    args.append(nc.dram_tensor("out_0", (B, S, D), F32, kind="ExternalOutput").ap())
    gated_block(nc, *args)
    r = _run(nc, [arrays], core_ids=[0])
    return r.results[0]["out_0"]
```

```python
from contextlib import ExitStack

import concourse.bass as bass
from concourse import mybir

ALU = mybir.AluOpType
ACT = mybir.ActivationFunctionType
F32 = mybir.dt.float32
BF16 = mybir.dt.bfloat16
U32 = mybir.dt.uint32
I32 = mybir.dt.int32
AX_X = mybir.AxisListType.X

P = 128
D = 128
H = 16
DK = D // H
S = 64
B = 128
N = B * S
UNIT = P
CU = 4
CT = CU * UNIT
NC_ = N // CT
NU = N // UNIT
GH = 8
G = H // GH
HR = P // GH
CJ = 4
EPS = 1e-5
ISC = float(DK) ** -0.5
NE = 8
GD = 16
HID = 256
HH = HID // P
NT = N // P + NE
RW = D + 4
R_RSTD, R_MEAN, R_GATE, R_ID = D, D + 1, D + 2, D + 3
ROWS = N + P
UA = CU * (NC_ - 4)
NB = 8


def gated_block(nc, x, ctx_in, g_xattn, g_ffn, W_q, b_q, W_k, b_k, W_v, b_v, W_o, b_o, w_red, wg, W1, b1, W2, b2, out):
    es = ExitStack()
    with es:
        def sb(name, shape, dt=F32):
            return es.enter_context(nc.sbuf_tensor(name, shape, dt))

        def pb(name, shape, dt=F32):
            return es.enter_context(nc.psum_tensor(name, shape, dt))

        def sem(name):
            return es.enter_context(nc.semaphore(name))

        x_t = x.rearrange("(t two) s d -> (two s) t d", two=2)
        c_t = ctx_in.rearrange("(t two) s d -> (two s) t d", two=2)
        out_rows = out.rearrange("b s d -> (b s) d")
        records = nc.dram_tensor("records", [NE * ROWS + P, RW], F32, kind="Internal").ap()

        ident = sb("ident", [P, P])
        w16 = sb("w16", [P, 2, G, GH, HR])
        wv = sb("wv", [P, D])
        wo = sb("wo", [P, 2, CJ, D])
        b16 = sb("b16", [P, 2, G])
        hmask = sb("hmask", [P, GH])
        one = sb("one", [1, 1])
        bv = sb("bv", [P, D])
        tgbo = sb("tgbo", [P, D])
        gx = sb("gx", [P, 1])
        tg = sb("tg", [P, 1])
        ksum = sb("ksum", [P, 32])
        mhalf = sb("mhalf", [P, CU])
        tri = sb("tri", [P, P], BF16)
        ones = sb("ones", [P, P], BF16)
        rank = sb("rank", [P, NE])
        ebase = sb("ebase", [P, NE])
        carry = sb("carry", [P, NE])
        oh = sb("oh", [P, NU, NE], BF16)
        blank = sb("blank", [P, RW])
        tgf = sb("tgf", [P, 1])
        gf = sb("gf", [P, 1])
        wred = sb("wred", [P, GD])
        wgs = sb("wgs", [NE, GD])
        wgn = sb("wgn", [NE, GD])
        wgT = sb("wgT", [GD, NE])
        nrm = sb("nrm", [NE, 4])
        wc = sb("wc", [P, NE])
        b1c = sb("b1c", [P, NE, HH])
        eid = sb("eid", [P, NT], I32)
        pos = sb("pos", [P, NU], U32)
        XR = sb("XR", [P, NU, RW])
        X = XR[:, :, 0:D]
        XC = [sb(f"XC{i}", [P, CU, D]) for i in range(2)]
        C = [sb(f"C{i}", [P, CU, D]) for i in range(2)]
        st = sb("st", [P, CU, 6])
        mv = sb("mv", [P, CU, 2])
        ve = sb("ve", [P, CU])
        rstd = sb("rstd", [P, CU])
        gst = sb("gst", [P, CU, 6])
        gmv = sb("gmv", [P, CU, 2])
        gve = sb("gve", [P, CU])
        grstd = sb("grstd", [P, CU])
        wmean = sb("wmean", [GD, 2])
        lg = sb("lg", [P, NU, NE])
        xn = sb("xn", [P, CU, D])
        xT = sb("xT", [P, CT])
        cT = sb("cT", [P, CT])
        Q16 = [sb(f"Q16{i}", [P, G, CT]) for i in range(2)]
        qb = sb("qb", [P, G, CT], BF16)
        kT = [sb(f"kT{i}", [P, G, CT]) for i in range(2)]
        kb = sb("kb", [P, G, CT], BF16)
        Kd = [sb(f"Kd{i}", [P, G, GH, CT], BF16) for i in range(2)]
        Qd = [sb(f"Qd{i}", [P, G, GH, CT]) for i in range(2)]
        V = [sb(f"V{i}", [P, CU, H, 32]) for i in range(2)]
        mx = sb("mx", [P, CU, G, GH, HR])
        PT = [sb(f"PT{i}", [P, H, S]) for i in range(2)]
        rec = sb("rec", [P, CJ * S])
        OT = [sb(f"OT{i}", [P, CJ, S]) for i in range(2)]

        key, ta, tb = (V[0][:, i].rearrange("p h r -> p (h r)").rearrange("p (u e) -> p u e", e=NE) for i in range(3))
        wq, wk, bo, b1s = (PT[0][:, 2 * i:2 * i + 2, :].rearrange("p h q -> p (h q)") for i in range(4))
        b1s = b1s[0:NE * HH, :]
        token = pos[:, :].bitcast(I32)
        wredT = PT[1][0:GD, 2 * G * P // S:2 * G * P // S + P // S, :].rearrange("p h q -> p (h q)")
        brow = PT[1][0:1, 0:2 * G * P // S, :].rearrange("p h q -> p (h q)").rearrange("p (i g h r) -> p i g h r", i=2, g=G, h=GH)
        wg2 = PT[1][0:NE, H - 1, 0:GD]
        small = PT[0][:, :, :].rearrange("p h q -> p (h q)")
        kd0 = Kd[0][:, :, :, :].rearrange("p g h t -> p (g h t)").bitcast(F32)
        kd1 = Kd[1][:, :, :, :].rearrange("p g h t -> p (g h t)").bitcast(F32)
        w1 = kd0[:, 0:NE * HID].rearrange("p (e h) -> p e h", e=NE)
        w2 = kd0[:, NE * HID:2 * NE * HID].rearrange("p (e m c) -> p e m c", e=NE, m=HH)
        b2r = kd1[0:1, 0:NE * D].rearrange("p (e c) -> p e c", e=NE)
        at = NE * D
        tile_no = kd1[:, at:at + NT]
        tile_i, row = (kd1[:, at + NT * i:at + NT * i + NT].bitcast(I32) for i in (1, 2))
        rsum, rowf = (kd1[:, at + NT * i:at + NT * i + NT] for i in (3, 4))
        bpos = kd1[:, at + 5 * NT:at + 5 * NT + NE].bitcast(I32)
        ones_row = kd1[0:1, at + 5 * NT + NE:at + 5 * NT + NE + P]
        early = [t[:, :, :].rearrange("p u d -> p (u d)") for t in (XC[0], C[0], xn)]
        qd0 = Qd[0][:, :, :, :].rearrange("p g h t -> p (g h t)")
        rr = [qd0[:, RW * i:RW * i + RW] for i in range(NB)]
        at = RW * NB
        fo = [qd0[:, at + D * i:at + D * i + D] for i in range(NB)]
        at += D * NB
        fx, fxT = ([qd0[:, at + D * (2 * k + i):at + D * (2 * k + i) + D] for i in range(2)] for k in range(2))
        at += 4 * D
        w1s = [qd0[:, at + HID * i:at + HID * i + HID] for i in range(2)]
        at += 2 * HID
        fh = [qd0[:, at + HID * i:at + HID * i + HID].rearrange("p (m t) -> p m t", m=HH) for i in range(2)]
        at += HID * 2
        b1t = [qd0[:, at + HH * i:at + HH * i + HH] for i in range(2)]
        cmpt = Qd[1][:, 0, 0:2, :].rearrange("p a b -> p (a b)")[:, 0:NT * NE].rearrange("p (t e) -> p t e", e=NE)

        s2p = [pb(f"s2p{i}", [P, 512]) for i in range(2)]
        s1p = [pb(f"s1p{i}", [P, 512]) for i in range(2)]
        pvp = pb("pvp", [P, 512])
        m0 = pb("m0", [P, 512])
        m1 = pb("m1", [P, 512])
        m2 = pb("m2", [P, 512])

        w_in = sem("w_in")
        memset_done = sem("memset_done")
        x_in = [sem(f"x_in{i}") for i in range(2)]
        c_in = [sem(f"c_in{i}") for i in range(2)]
        kd_in = [sem(f"kd_in{i}") for i in range(2)]
        qm_ok = sem("qm_ok")
        qd_v = sem("qd_v")
        qd_a = sem("qd_a")
        setup_v = sem("setup_v")
        setup_a = sem("setup_a")
        setup_p = sem("setup_p")
        setup_t = sem("setup_t")
        stats = sem("stats")
        stat_step = sem("stat_step")
        rstd_ok = sem("rstd_ok")
        pool_step = sem("pool_step")
        xn_ok = sem("xn_ok")
        xb_ok = sem("xb_ok")
        xT_ps = sem("xT_ps")
        cT_ps = sem("cT_ps")
        xT_sb = sem("xT_sb")
        cT_sb = sem("cT_sb")
        q_ps = sem("q_ps")
        k_ps = sem("k_ps")
        v_ps = sem("v_ps")
        q_sb = sem("q_sb")
        k_sb = sem("k_sb")
        qb_ok = sem("qb_ok")
        kb_ok = sem("kb_ok")
        v_sb = sem("v_sb")
        s1_ps = sem("s1_ps")
        mx_ok = sem("mx_ok")
        mT_ps = sem("mT_ps")
        s2_ps = sem("s2_ps")
        pt_ok = sem("pt_ok")
        pv_ps = sem("pv_ps")
        rec_ok = sem("rec_ok")
        ot_ok = sem("ot_ok")
        o_ps = sem("o_ps")
        x1_ok = sem("x1_ok")
        hm_ok = sem("hm_ok")
        fill_ok = sem("fill_ok")
        passed = sem("passed")
        we_in = sem("we_in")
        nrm_ok = sem("nrm_ok")
        wgn_ok = sem("wgn_ok")
        wgT_ok = sem("wgT_ok")
        wc_ok = sem("wc_ok")
        chain = sem("chain")
        pchain = sem("pchain")
        gs1 = sem("gs1")
        g_stat = sem("g_stat")
        g_rstd = sem("g_rstd")
        g_cp = sem("g_cp")
        g_pay = sem("g_pay")
        g_tr = sem("g_tr")
        g_xT = sem("g_xT")
        g_lg = sem("g_lg")
        g_lgv = sem("g_lgv")
        diff_ok = sem("diff_ok")
        ex_ok = sem("ex_ok")
        oh_ok = sem("oh_ok")
        cnt_ps = sem("cnt_ps")
        cnt_rd = sem("cnt_rd")
        row_ok = sem("row_ok")
        bpos_ok = sem("bpos_ok")
        tile_ok = sem("tile_ok")
        pos_ok = sem("pos_ok")
        eid_ok = sem("eid_ok")
        gate_ok = sem("gate_ok")
        rec_out = sem("rec_out")
        blank_out = sem("blank_out")
        r_in = [sem(f"r_in{i}") for i in range(NB)]
        f_xn = sem("f_xn")
        f_tr = sem("f_tr")
        f_xT = sem("f_xT")
        f_w = sem("f_w")
        f_h = sem("f_h")
        f_g = sem("f_g")
        f_o = sem("f_o")
        f_out = sem("f_out")
        scat = [sem(f"scat{i}") for i in range(NB)]
        NW = 5 + 2 * CJ + 3 + 4

        def steps(eng, step):
            def at(s):
                step(s, s % 2, s < NC_, 1 <= s <= NC_, 2 <= s <= NC_ + 1, s >= 3)
            for s in range(4):
                at(s)
            with eng.Fori(2, NC_ // 2 - 1, 1) as i:
                for p in range(2):
                    step(2 * i + p, p, True, True, True, True)
            for s in range(NC_ - 2, NC_ + 3):
                at(s)

        def settle(eng):
            eng.sem_inc(passed, 1)

        def kd_count(s, p):
            return 256 * ((s + 1) // 2) if isinstance(s, int) else 128 * (s + p)

        def tiles(eng, step):
            for k in range(NB):
                step(k, k, min(k, 2), True)
            with eng.Fori(1, NT // NB, 1) as i:
                for q in range(NB):
                    step(NB * i + q, q, 2, True)
            for k in range(NT, NT + 2):
                step(k, k % NB, 3 if k > NT else 2, False)

        block = es.enter_context(nc.Block())

        @block.sync
        def _(sp):
            sp.wait_ge(memset_done, 1)
            sp.dma_start(wq[:, :], W_q).then_inc(w_in, 16)
            sp.dma_start(wk[:, :], W_k).then_inc(w_in, 16)
            sp.dma_start(wv[:, :], W_v).then_inc(w_in, 16)
            for i, b_ in enumerate((b_q, b_k)):
                sp.dma_start(brow[:, i, :, :, 0:DK], b_.rearrange("(o g h d) -> o g h d", o=1, g=G, h=GH)).then_inc(w_in, 16)
            for b in range(2):
                for j in range(CJ):
                    r = 32 * j + HR * b
                    sp.dma_start(wo[r:r + DK, b], W_o.rearrange("(j g d) n -> j d g n", j=CJ, g=4)[j]).then_inc(w_in, 16)
            sp.dma_start(bv[:, :], b_v.rearrange("(o n) -> o n", o=1).to_broadcast([P, D])).then_inc(w_in, 16)
            sp.dma_start(bo[:, :], b_o.rearrange("(o n) -> o n", o=1).to_broadcast([P, D])).then_inc(w_in, 16)
            sp.dma_start(gx[:, :], g_xattn.rearrange("(o n) -> o n", o=1).to_broadcast([P, 1])).then_inc(w_in, 16)
            sp.dma_start(gf[:, :], g_ffn.rearrange("(o n) -> o n", o=1).to_broadcast([P, 1])).then_inc(w_in, 16)
            sp.dma_start(wred[:, :], w_red).then_inc(w_in, 16)
            sp.dma_start(wgs[:, :], wg).then_inc(w_in, 16)
            sp.dma_start(b1s[:, :], b1.rearrange("e (m p) -> (e m) p", m=HH)).then_inc(w_in, 16)
            for c in range(2):
                sp.dma_start(XC[c][:, :, :], x_t[:, CU * c:CU * c + CU]).then_inc(x_in[c], 16)
                sp.dma_start(C[c][:, :, :], c_t[:, CU * c:CU * c + CU]).then_inc(c_in[c], 16)

            def step(s, p, proj, peak, attend, gate):
                if not isinstance(s, int) or s + 2 < NC_:
                    sp.wait_ge(cT_ps, s + 1)
                    cu = bass.ds(CU * (s + 2), CU)
                    sp.dma_start(C[p][:, :, :], c_t[:, cu]).then_inc(c_in[p], 16)
                if proj:
                    if isinstance(s, int) and s == 0:
                        sp.wait_ge(memset_done, 2)
                    if not isinstance(s, int) or s >= 2:
                        sp.wait_ge(s1_ps, 2 * CU * (s - 1))
                    sp.wait_ge(kb_ok, 2 * s + 2)
                    for g in range(G):
                        for h in range(GH):
                            r = slice(HR * h, HR * h + DK)
                            sp.dma_start(Kd[p][r, g, h, :], kb[r, g, :]).then_inc(kd_in[p], 16)
                if not isinstance(s, int) or s + 2 < NC_:
                    if gate:
                        sp.wait_ge(g_tr, s - 2)
                    else:
                        sp.wait_ge(xb_ok, s + 1)
                    sp.dma_start(XC[p][:, :, :], x_t[:, cu]).then_inc(x_in[p], 16)
            steps(sp, step)
            sp.wait_ge(s1_ps, 2 * NU)
            sp.dma_start(w1[:, :, :], W1.rearrange("e c h -> c e h")).then_inc(we_in, 16)
            for e in range(NE):
                sp.dma_start(w2[:, e], W2.rearrange("e (m p) c -> e p m c", m=HH)[e]).then_inc(we_in, 16)
            sp.dma_start(b2r, b2.rearrange("(o e) c -> o e c", o=1)).then_inc(we_in, 16)
            sp.wait_ge(bpos_ok, 1)
            for e in range(NE):
                r = sp.value_load(bpos[0:1, e:e + 1], min_val=0, max_val=NE * ROWS)
                sp.dma_start(records[bass.ds(r, P), :], blank[:, :]).then_inc(blank_out, 16)
            sp.wait_ge(fill_ok, 16)
            sp.wait_ge(blank_out, 16 * NE)
            sp.wait_ge(rec_out, 16 * NU)
            sp.wait_ge(row_ok, 1)

            def load(i, q):
                if not isinstance(i, int):
                    sp.wait_ge(scat[q], (i - q) * (16 // NB))
                    settle(sp)
                r = sp.value_load(row[0:1, bass.ds(i, 1)], min_val=0, max_val=NE * ROWS)
                sp.dma_start(rr[q], records[bass.ds(r, P), :]).then_inc(r_in[q], 16)
            for q in range(NB):
                load(q, q)
            with sp.Fori(1, NT // NB, 1) as k:
                for q in range(NB):
                    load(NB * k + q, q)
            for q in range(NB):
                sp.wait_ge(scat[q], 16 * (NT // NB))

        @block.gpsimd
        def _(pool):
            nc.gpsimd.memset(brow[:, :, :, :, :], 0.0).then_inc(pool_step, 1)
            nc.gpsimd.memset(one[:, :], 1.0)
            nc.gpsimd.memset(mhalf[:, :], -0.5)
            nc.gpsimd.memset(wo[:, :, :, :], 0.0)
            pool.wait_ge(pool_step, 1)
            nc.gpsimd.memset(brow[:, 1, :, :, DK:DK + 1], 1.0).then_inc(memset_done, 1)
            nc.gpsimd.memset(ident[:, :], 0.0).then_inc(pool_step, 1)
            pool.wait_ge(pool_step, 2)
            nc.gpsimd.affine_select(out=ident[:, :], in_=ident[:, :], compare_op=ALU.not_equal, fill=1.0, base=0,
                                    pattern=[[-1, P]], channel_multiplier=1).then_inc(setup_p, 1)
            nc.gpsimd.memset(V[0][:, :, :, :], 0.0)
            nc.gpsimd.memset(V[1][:, :, :, :], 0.0).then_inc(setup_p, 1)
            nc.gpsimd.memset(mx[:, :, :, :, :], 0.0)
            nc.gpsimd.memset(Kd[0][:, :, :, :].bitcast(U32), 0)
            nc.gpsimd.memset(Kd[1][:, :, :, :].bitcast(U32), 0).then_inc(memset_done, 1)
            nc.gpsimd.memset(hmask[:, :], 1.0).then_inc(hm_ok, 1)
            pool.wait_ge(hm_ok, 1)
            nc.gpsimd.affine_select(out=hmask[:, :], in_=hmask[:, :], compare_op=ALU.is_ge, fill=0.0, base=0,
                                    pattern=[[-HR, GH]], channel_multiplier=1).then_inc(hm_ok, 1)
            pool.wait_ge(hm_ok, 2)
            nc.gpsimd.affine_select(out=hmask[:, :], in_=hmask[:, :], compare_op=ALU.is_ge, fill=0.0, base=HR - 1,
                                    pattern=[[HR, GH]], channel_multiplier=-1).then_inc(hm_ok, 1)
            nc.gpsimd.memset(tri[:, :], 1.0)
            nc.gpsimd.memset(ones[:, :], 1.0)
            nc.gpsimd.memset(blank[:, :], 0.0)
            for e in range(NE):
                nc.gpsimd.memset(rank[:, e:e + 1], float(NE - e))
                nc.gpsimd.memset(ebase[:, e:e + 1], float(ROWS * e))
            nc.gpsimd.iota(token[:, :], pattern=[[P, NU]], base=0, channel_multiplier=1).then_inc(pchain, 1)
            pool.wait_ge(pchain, 1)
            nc.gpsimd.affine_select(out=tri[:, :], in_=tri[:, :], compare_op=ALU.is_gt, fill=0.0, base=0,
                                    pattern=[[1, P]], channel_multiplier=-1)
            nc.gpsimd.tensor_copy(XR[:, :, R_ID].bitcast(I32), token[:, :])
            nc.gpsimd.memset(blank[:, R_ID:R_ID + 1].bitcast(I32), N).then_inc(pchain, 1)
            pool.wait_ge(pchain, 2)
            pool.dma_start(records[NE * ROWS:NE * ROWS + P, :], blank[:, :]).then_inc(fill_ok, 16)
            pool.wait_ge(nrm_ok, 1)
            nc.gpsimd.tensor_tensor(nrm[:, 1:2], nrm[:, 0:1], nrm[:, 3:4], ALU.pow).then_inc(nrm_ok, 1)
            pool.wait_ge(setup_a, 1)
            pool.wait_ge(w_in, 16 * NW)
            nc.gpsimd.tensor_scalar(tgbo[:, :], bo[:, :], tg[:, 0:1], None, ALU.mult).then_inc(pool_step, 1)
            pool.wait_ge(pool_step, 3)

            def norm(c, p):
                pool.wait_ge(stats, c + 1)
                nc.gpsimd.tensor_tensor(rstd[:, :], ve[:, :], mhalf[:, :], ALU.pow).then_inc(rstd_ok, 1)
                pool.wait_ge(rstd_ok, c + 1)
                if not isinstance(c, int) or c >= 1:
                    pool.wait_ge(xT_ps, c)
                settle(pool)
                for u in range(CU):
                    i = nc.gpsimd.tensor_scalar(xn[:, u, :], XC[p][:, u, :],
                                                mv[:, u, 0:1], rstd[:, u:u + 1], ALU.subtract, ALU.mult)
                i.then_inc(xn_ok, 1)
                for u in range(CU):
                    i = nc.gpsimd.tensor_tensor(X[:, bass.ds(CU * c + u, 1), :].rearrange("p o d -> p (o d)"),
                                                XC[p][:, u, :], tgbo[:, :], ALU.add)
                i.then_inc(xb_ok, 1)

            norm(0, 0)

            def gate_norm(c):
                pool.wait_ge(g_stat, c + 1)
                nc.gpsimd.tensor_tensor(grstd[:, :], gve[:, :], mhalf[:, :], ALU.pow).then_inc(g_rstd, 1)
                pool.wait_ge(g_rstd, c + 1)
                settle(pool)
                nc.gpsimd.tensor_copy(XR[:, bass.ds(CU * c, CU), R_MEAN], gmv[:, :, 0])
                nc.gpsimd.tensor_copy(XR[:, bass.ds(CU * c, CU), R_RSTD], grstd[:, :]).then_inc(g_pay, 1)

            def send(first, last):
                for u in range(first, last):
                    nc.gpsimd.indirect_dma_start(out=records, out_offset=bass.IndirectOffsetOnAxis(ap=pos[:, u:u + 1], axis=0),
                                                 in_=XR[:, u, :], in_offset=None).then_inc(rec_out, 16)

            def step(s, p, proj, peak, attend, gate):
                if gate:
                    if proj:
                        pool.wait_ge(xb_ok, s + 1)
                    else:
                        pool.wait_ge(g_tr, s - 4)
                    pool.wait_ge(x1_ok, CU * (s - 2))
                    settle(pool)
                    nc.gpsimd.tensor_copy(XC[p][:, :, :], X[:, bass.ds(CU * (s - 3), CU), :]).then_inc(g_cp, 1)
                    gate_norm(s - 3)
                if proj and (not isinstance(s, int) or s + 1 < NC_):
                    norm(s + 1, 1 - p)
                if isinstance(s, int) and NC_ - 1 <= s < NC_ + 2:
                    pool.wait_ge(pos_ok, 1)
                    pool.wait_ge(gate_ok, 1)
                    k = s - NC_ + 1
                    send(UA // 3 * k, UA // 3 * (k + 1))
            steps(pool, step)

            pool.wait_ge(s1_ps, 2 * NU)
            nc.gpsimd.memset(ones_row, 1.0)
            nc.gpsimd.iota(tile_i, pattern=[[1, NT]], base=0, channel_multiplier=0).then_inc(tile_ok, 1)
            pool.wait_ge(tile_ok, 1)
            nc.gpsimd.tensor_copy(tile_no, tile_i).then_inc(tile_ok, 1)
            pool.wait_ge(pos_ok, 2)
            pool.wait_ge(gate_ok, 2)
            send(UA, NU)

            def scatter(i, q):
                pool.wait_ge(f_out, i + 1)
                settle(pool)
                nc.gpsimd.indirect_dma_start(
                    out=out_rows, out_offset=bass.IndirectOffsetOnAxis(ap=rr[q][:, R_ID:R_ID + 1].bitcast(U32), axis=0),
                    in_=fo[q], in_offset=None, bounds_check=N - 1, oob_is_err=False).then_inc(scat[q], 16)
            def tstep(k, q, head, tail):
                if head >= 2:
                    scatter(k - 2, (q + NB - 2) % NB)
            tiles(pool, tstep)

        @block.scalar
        def _(act):
            act.wait_ge(w_in, 16 * NW)
            nc.scalar.activation(tg[:, :], gx[:, :], ACT.Tanh).then_inc(setup_a, 1)
            act.wait_ge(setup_t, 1)
            nc.scalar.mul(b16[:, 0, :], m0[:, 0:G], ISC).then_inc(setup_a, 1)
            nc.scalar.activation(b16[:, 1, :], m0[:, G:2 * G], ACT.Copy).then_inc(setup_a, 1)
            act.wait_ge(setup_a, 3)
            nc.scalar.activation(tgf[:, :], gf[:, :], ACT.Tanh).then_inc(setup_a, 1)

            def gate_exp(first, last, k):
                act.wait_ge(diff_ok, k)
                nc.scalar.activation(lg[:, first:last, :], lg[:, first:last, :], ACT.Exp).then_inc(ex_ok, 1)

            def exp(s, u):
                c = s - 2
                for g in range(G):
                    act.wait_ge(s2_ps, 2 * CU * c + 2 * u + g + 1)
                    if u < 2:
                        if not isinstance(s, int) or s >= 3:
                            act.wait_ge(pv_ps, CU * c + u - 1)
                    else:
                        act.wait_ge(pv_ps, CU * c + u - 1)
                    nc.scalar.activation(PT[u % 2][:, GH * g:GH * g + GH, :], s2p[g][:, :].rearrange("p (h q) -> p h q", h=GH),
                                         ACT.Exp).then_inc(pt_ok, 1)

            def step(s, p, proj, peak, attend, gate):
                if proj:
                    act.wait_ge(xT_ps, s + 1)
                    nc.scalar.activation(xT[:, :], m0[:, :], ACT.Copy).then_inc(xT_sb, 1)
                    act.wait_ge(cT_ps, s + 1)
                    if not isinstance(s, int) or s >= 4:
                        act.wait_ge(g_lg, s - 3)
                    nc.scalar.activation(cT[:, :], m1[:, :], ACT.Copy).then_inc(cT_sb, 1)
                if attend:
                    exp(s, 0)
                if proj:
                    if not isinstance(s, int) or s >= 1:
                        act.wait_ge(kd_in[1 - p], kd_count(s, p))
                    for g, m in enumerate((m0, m1)):
                        act.wait_ge(k_ps, 2 * s + g + 1)
                        nc.scalar.activation(kb[:, g, :], m[:, :], ACT.Identity, bias=b16[:, 1, g:g + 1]).then_inc(kb_ok, 1)
                if isinstance(s, int) and s == NC_ - 1:
                    gate_exp(0, UA, 1)
                if attend:
                    for u in range(1, CU):
                        exp(s, u)
                if proj:
                    for g, m in enumerate((m0, m1)):
                        nc.scalar.activation(kT[p][:, g, :], m[:, :], ACT.Identity, bias=b16[:, 1, g:g + 1]).then_inc(k_sb, 1)
                if gate:
                    act.wait_ge(g_tr, s - 2)
                    nc.scalar.activation(cT[:, :], m1[:, :], ACT.Copy).then_inc(g_xT, 1)
                if peak:
                    if isinstance(s, int) and s == 1:
                        act.wait_ge(hm_ok, 3)
                    act.wait_ge(qm_ok, 2 * s)
                    for h in range(1, GH):
                        a = nc.scalar.activation(Qd[1 - p][:, 1, h, :], Q16[1 - p][:, 1, :], ACT.Copy, scale=hmask[:, h:h + 1])
                    a.then_inc(qd_a, 1)
                if proj:
                    for g, m in enumerate(s1p):
                        act.wait_ge(q_ps, 2 * s + g + 1)
                        nc.scalar.activation(qb[:, g, :], m[:, :], ACT.Identity, bias=b16[:, 0, g:g + 1],
                                             scale=ISC).then_inc(qb_ok, 1)
                    for g, m in enumerate(s1p):
                        nc.scalar.activation(Q16[p][:, g, :], m[:, :], ACT.Identity, bias=b16[:, 0, g:g + 1],
                                             scale=ISC).then_inc(q_sb, 1)
            steps(act, step)

            gate_exp(UA, NU, 2)

            act.wait_ge(eid_ok, 1)
            act.wait_ge(we_in, 16 * (2 + NE))

            def stage(k, q):
                p = q % 2
                e = act.value_load(eid[0:1, bass.ds(k, 1)], min_val=0, max_val=NE - 1)
                if not isinstance(k, int) or k >= 2:
                    act.wait_ge(f_g, k - 1)
                nc.scalar.activation(w1s[p], w1[:, bass.ds(e, 1), :].rearrange("p o h -> p (o h)"), ACT.Copy)
                nc.scalar.activation(b1t[p], b1c[:, bass.ds(e, 1), :].rearrange("p o m -> p (o m)"), ACT.Copy).then_inc(f_w, 1)

            def tstep(k, q, head, tail):
                if tail:
                    stage(k, q)
                if head >= 1 and (tail or k == NT):
                    i, p = k - 1, 1 - q % 2
                    act.wait_ge(f_h, i + 1)
                    for m in range(HH):
                        a = nc.scalar.activation(fh[p][:, m, :], s1p[p][:, P * m:P * m + P], ACT.Gelu, bias=b1t[p][:, m:m + 1])
                    a.then_inc(f_g, 1)
            tiles(act, tstep)

        @block.vector
        def _(dve):
            nc.vector.memset(ksum[:, :], 0.0).then_inc(setup_v, 1)
            dve.wait_ge(setup_v, 1)
            nc.vector.memset(ksum[0:S, 0:HR], 1.0)
            nc.vector.memset(ksum[S:P, HR:2 * HR], 1.0)
            nc.vector.memset(w16[:, :, :, :, :], 0.0).then_inc(setup_v, 1)
            dve.wait_ge(setup_v, 2)
            dve.wait_ge(w_in, 16 * NW)
            nc.vector.tensor_copy(w16[:, 0, :, :, 0:DK], wq[:, :].rearrange("p (g h d) -> p g h d", g=G, h=GH))
            nc.vector.tensor_copy(w16[:, 1, :, :, 0:DK], wk[:, :].rearrange("p (g h d) -> p g h d", g=G, h=GH)).then_inc(setup_v, 1)

            def stat(c, p):
                dve.wait_ge(x_in[p], 16 * (c // 2) + 16 if isinstance(c, int) else 8 * (c - p) + 16)
                if not isinstance(c, int) or c >= 1:
                    dve.wait_ge(xn_ok, c)
                for u in range(CU):
                    i = nc.vector.bn_stats(st[:, u, :], XC[p][:, u, :])
                i.then_inc(stat_step, 1)
                dve.wait_ge(stat_step, 2 * c + 1)
                settle(dve)
                for u in range(CU):
                    i = nc.vector.bn_aggr(mv[:, u, :], st[:, u, :])
                i.then_inc(stat_step, 1)
                dve.wait_ge(stat_step, 2 * c + 2)
                nc.vector.tensor_scalar_add(ve[:, :], mv[:, :, 1], EPS).then_inc(stats, 1)

            def peak_of(s, u):
                for g in range(G):
                    dve.wait_ge(s1_ps, 2 * CU * (s - 1) + 2 * u + g + 1)
                    if u == 0 and g == 0 and (not isinstance(s, int) or s >= 2):
                        dve.wait_ge(mT_ps, 2 * s - 2)
                    nc.vector.tensor_reduce(mx[:, u, g, :, DK], s1p[g][:, :].rearrange("p (h k) -> p h k", h=GH),
                                            AX_X, ALU.max).then_inc(mx_ok, 1)

            def norm_of(s, u):
                n = CU * (s - 2) + u
                dve.wait_ge(pv_ps, n + 1)
                nc.vector.reciprocal(rec[:, :], pvp[:, CJ * S:2 * CJ * S]).then_inc(rec_ok, 1)
                dve.wait_ge(rec_ok, n + 1)
                if u >= 2 or not isinstance(s, int) or s >= 3:
                    dve.wait_ge(o_ps, n - 1)
                nc.vector.tensor_tensor(OT[u % 2][:, :, :].rearrange("p g q -> p (g q)"), pvp[:, 0:CJ * S], rec[:, :],
                                        ALU.mult).then_inc(ot_ok, 1)

            def x1_of(s, u):
                n = CU * (s - 2) + u
                dve.wait_ge(o_ps, n + 1)
                dve.wait_ge(xb_ok, s - 1)
                xu = X[:, bass.ds(n, 1), :].rearrange("p o d -> p (o d)")
                nc.vector.scalar_tensor_tensor(out=xu, in0=m2[:, 0:D], scalar=tg[:, 0:1], in1=xu,
                                               op0=ALU.mult, op1=ALU.add).then_inc(x1_ok, 1)

            vc = [0]

            def link(i):
                vc[0] += 1
                i.then_inc(chain, 1)
                dve.wait_ge(chain, vc[0])

            nc.vector.memset(nrm[:, 3:4], 0.5)
            link(nc.vector.tensor_tensor(wg2, wgs[:, :], wgs[:, :], ALU.mult))
            nc.vector.tensor_reduce(nrm[:, 0:1], wg2, AX_X, ALU.add).then_inc(nrm_ok, 1)
            dve.wait_ge(nrm_ok, 2)
            link(nc.vector.tensor_scalar_max(nrm[:, 2:3], nrm[:, 1:2], 1e-4))
            link(nc.vector.reciprocal(nrm[:, 0:1], nrm[:, 2:3]))
            nc.vector.tensor_scalar(wgn[:, :], wgs[:, :], nrm[:, 0:1], None, ALU.mult).then_inc(wgn_ok, 1)
            dve.wait_ge(setup_t, 2)
            nc.vector.tensor_copy(b1c[:, :, :].rearrange("p e m -> p (e m)"), s1p[0][:, 0:NE * HH])
            link(nc.vector.tensor_copy(wredT[:, :], m1[0:GD, 0:P]))
            link(nc.vector.tensor_reduce(wmean[:, 0:1], wredT[:, :], AX_X, ALU.add))
            link(nc.vector.tensor_scalar_mul(wmean[:, 1:2], wmean[:, 0:1], 1.0 / D))
            nc.vector.tensor_scalar(wredT[:, :], wredT[:, :], wmean[:, 1:2], None, ALU.subtract).then_inc(wgT_ok, 1)
            dve.wait_ge(setup_t, 3)
            nc.vector.tensor_copy(wgT[:, :], m2[0:GD, 0:NE]).then_inc(wgT_ok, 1)
            dve.wait_ge(setup_t, 4)
            nc.vector.tensor_copy(wc[:, :], pvp[:, 0:NE]).then_inc(wc_ok, 1)

            def gate_stat(c):
                dve.wait_ge(x1_ok, CU * c + CU)
                if not isinstance(c, int) or c >= 1:
                    dve.wait_ge(g_pay, c)
                settle(dve)
                for u in range(CU):
                    i = nc.vector.bn_stats(gst[:, u, :], X[:, bass.ds(CU * c + u, 1), :].rearrange("p o d -> p (o d)"))
                i.then_inc(gs1, 1)
                dve.wait_ge(gs1, 2 * c + 1)
                settle(dve)
                for u in range(CU):
                    i = nc.vector.bn_aggr(gmv[:, u, :], gst[:, u, :])
                i.then_inc(gs1, 1)
                dve.wait_ge(gs1, 2 * c + 2)
                nc.vector.tensor_scalar_add(gve[:, :], gmv[:, :, 1], EPS).then_inc(g_stat, 1)

            def gate_keep(c):
                dve.wait_ge(g_lg, c + 1)
                dve.wait_ge(g_pay, c + 1)
                cu = bass.ds(CU * c, CU)
                nc.vector.tensor_tensor(lg[:, cu, :], pvp[:, 0:CU * NE].rearrange("p (u e) -> p u e", e=NE),
                                        XR[:, cu, R_RSTD:R_RSTD + 1].to_broadcast([P, CU, NE]), ALU.mult).then_inc(g_lgv, 1)

            def route(first, last, k, ky, ta, tb, cols):
                n = last - first
                ky, ta, tb, cols = ky[:, 0:n, :], ta[:, 0:n, :], tb[:, 0:n, :], [c[:, 0:n] for c in cols]
                ex, o = lg[:, first:last, :], oh[:, first:last, :]

                def wide(ap):
                    return ap.rearrange("p (u o) -> p u o", o=1).to_broadcast([P, n, NE])

                def per_expert(ap):
                    return ap.rearrange("p (o e) -> p o e", o=1).to_broadcast([P, n, NE])

                dve.wait_ge(g_lgv, last // CU)
                link(nc.vector.tensor_reduce(cols[0], ex, AX_X, ALU.max))
                nc.vector.tensor_tensor(ex, ex, wide(cols[0]), ALU.subtract).then_inc(diff_ok, 1)
                dve.wait_ge(ex_ok, k)
                nc.vector.tensor_reduce(cols[1], ex, AX_X, ALU.add)
                link(nc.vector.tensor_reduce(cols[2], ex, AX_X, ALU.max))
                link(nc.vector.reciprocal(cols[3], cols[1]))
                link(nc.vector.tensor_tensor(cols[4], cols[2], cols[3], ALU.mult))
                dve.wait_ge(setup_a, 4)
                nc.vector.tensor_scalar(XR[:, first:last, R_GATE], cols[4], tgf[:, 0:1], None, ALU.mult).then_inc(gate_ok, 1)
                link(nc.vector.tensor_tensor(ky, ex, wide(cols[2]), ALU.is_equal))
                link(nc.vector.tensor_tensor(ky, ky, per_expert(rank[:, :]), ALU.mult))
                link(nc.vector.tensor_reduce(cols[5], ky, AX_X, ALU.max))
                nc.vector.tensor_tensor(o, ky, wide(cols[5]), ALU.is_equal).then_inc(oh_ok, 1)
                dve.wait_ge(cnt_ps, 2 * k)
                inside, tot = ex, ky
                nc.vector.tensor_copy(inside, pvp[:, 0:n * NE].rearrange("p (u e) -> p u e", e=NE))
                nc.vector.tensor_copy(tot, m2[:, 0:n * NE].rearrange("p (u e) -> p u e", e=NE))
                nc.vector.tensor_copy(ta, m2[:, 0:n * NE].rearrange("p (u e) -> p u e", e=NE)).then_inc(cnt_rd, 1)
                dve.wait_ge(cnt_rd, k)
                a, b, w = ta, tb, 1
                while w < n:
                    nc.vector.tensor_copy(b[:, 0:w, :], a[:, 0:w, :])
                    link(nc.vector.tensor_tensor(b[:, w:n, :], a[:, w:n, :], a[:, 0:n - w, :], ALU.add))
                    a, b, w = b, a, 2 * w
                if k == 1:
                    nc.vector.tensor_copy(carry[:, :], a[:, n - 1, :])
                else:
                    link(nc.vector.tensor_tensor(a, a, per_expert(carry[:, :]), ALU.add))
                link(nc.vector.tensor_tensor(b, a, tot, ALU.subtract))
                link(nc.vector.tensor_tensor(b, b, per_expert(ebase[:, :]), ALU.add))
                link(nc.vector.tensor_tensor(b, b, inside, ALU.add))
                link(nc.vector.tensor_tensor(b, b, o, ALU.mult))
                link(nc.vector.tensor_reduce(cols[1], b, AX_X, ALU.add))
                nc.vector.tensor_copy(pos[:, first:last], cols[1]).then_inc(pos_ok, 1)
                return a[:, n - 1, :]

            stat(0, 0)

            def step(s, p, proj, peak, attend, gate):
                if peak:
                    peak_of(s, 0)
                if gate:
                    gate_stat(s - 3)
                if peak:
                    peak_of(s, 1)
                if isinstance(s, int) and s == NC_ - 1:
                    dve.wait_ge(xb_ok, s)
                    dve.wait_ge(g_tr, s - 3)
                    dve.wait_ge(cT_ps, s)
                    dve.wait_ge(xT_ps, s + 1)
                    m = UA * NE
                    route(0, UA, 1, *[t[:, 0:m].rearrange("p (u e) -> p u e", e=NE) for t in early],
                          [early[i // 2][:, m + UA * (i % 2):m + UA * (i % 2) + UA] for i in range(6)])
                if peak:
                    peak_of(s, 2)
                if attend:
                    norm_of(s, 0)
                    norm_of(s, 1)
                if proj and (not isinstance(s, int) or s + 1 < NC_):
                    stat(s + 1, 1 - p)
                if peak:
                    peak_of(s, 3)
                if attend:
                    x1_of(s, 0)
                    norm_of(s, 2)
                    x1_of(s, 1)
                if peak:
                    for g, m in enumerate(s1p):
                        dve.wait_ge(mT_ps, 2 * (s - 1) + g + 1)
                        nc.vector.tensor_tensor(Q16[1 - p][:, g, :], Q16[1 - p][:, g, :], m[:, :],
                                                ALU.subtract).then_inc(qm_ok, 1)
                if attend:
                    norm_of(s, 3)
                if proj:
                    dve.wait_ge(v_ps, s + 1)
                    if isinstance(s, int) and s < 2:
                        dve.wait_ge(setup_p, 2)
                    for b in range(2):
                        r = slice(S * b, S * b + S)
                        i = nc.vector.tensor_tensor(
                            V[p][r, :, :, HR * b:HR * b + DK],
                            m0[r, :].rearrange("p (u h d) -> p u h d", u=CU, h=H),
                            bv[r, :].rearrange("p (o h d) -> p o h d", o=1, h=H).to_broadcast([S, CU, H, DK]), ALU.add)
                    i.then_inc(v_sb, 1)
                if attend:
                    x1_of(s, 2)
                if peak:
                    dve.wait_ge(qm_ok, 2 * s)
                    if isinstance(s, int) and s == 1:
                        dve.wait_ge(hm_ok, 3)
                    for h in range(GH):
                        i = nc.vector.tensor_scalar(Qd[1 - p][:, 0, h, :], Q16[1 - p][:, 0, :], hmask[:, h:h + 1], None, ALU.mult)
                    i = nc.vector.tensor_scalar(Qd[1 - p][:, 1, 0, :], Q16[1 - p][:, 1, :], hmask[:, 0:1], None, ALU.mult)
                    i.then_inc(qd_v, 1)
                if attend:
                    x1_of(s, 3)
                if gate:
                    gate_keep(s - 3)
            steps(dve, step)

            wide_col = [small[:, i * NU:i * NU + NU] for i in range(6)]
            total = route(UA, NU, 2, key, ta, tb, wide_col)
            tl = lambda n: small[:, (6 + n) * NU:(6 + n) * NU + NE]
            nc.vector.tensor_tensor(bpos, total, ebase[:, :], ALU.add).then_inc(bpos_ok, 1)
            link(nc.vector.tensor_scalar_add(tl(0).bitcast(I32), total, float(P - 1)))
            link(nc.vector.tensor_single_scalar(tl(1).bitcast(I32), tl(0).bitcast(I32), 7, ALU.arith_shift_right))
            nc.vector.tensor_copy(tl(2), tl(1).bitcast(I32))
            link(nc.vector.tensor_copy(tl(3), tl(1).bitcast(I32)))
            c, d, k = 3, 4, 1
            while k < NE:
                nc.vector.tensor_copy(tl(d)[:, 0:k], tl(c)[:, 0:k])
                link(nc.vector.tensor_tensor(tl(d)[:, k:NE], tl(c)[:, k:NE], tl(c)[:, 0:NE - k], ALU.add))
                c, d, k = d, c, 2 * k
            link(nc.vector.tensor_scalar(tl(5), tl(2), float(-P), float(ROWS), ALU.mult, ALU.add))
            dve.wait_ge(tile_ok, 2)
            link(nc.vector.tensor_tensor(
                cmpt, tl(c).rearrange("p (o e) -> p o e", o=1).to_broadcast([P, NT, NE]),
                tile_no.rearrange("p (t o) -> p t o", o=1).to_broadcast([P, NT, NE]), ALU.is_le))
            cnt = Qd[1][:, 0, 2, 0:NT]
            link(nc.vector.tensor_reduce(cnt, cmpt, AX_X, ALU.add))
            nc.vector.tensor_scalar_min(eid[:, :], cnt, float(NE - 1)).then_inc(eid_ok, 1)
            link(nc.vector.tensor_tensor(cmpt, cmpt, tl(5).rearrange("p (o e) -> p o e", o=1).to_broadcast([P, NT, NE]), ALU.mult))
            nc.vector.tensor_scalar_mul(rowf, tile_no, float(P))
            link(nc.vector.tensor_reduce(rsum, cmpt, AX_X, ALU.add))
            link(nc.vector.tensor_tensor(rowf, rowf, rsum, ALU.add))
            nc.vector.tensor_scalar_min(row, rowf, float(NE * ROWS)).then_inc(row_ok, 1)
            dve.wait_ge(eid_ok, 1)
            dve.wait_ge(we_in, 16 * (2 + NE))

            def ft_norm(i, q):
                p = q % 2
                if isinstance(i, int):
                    dve.wait_ge(r_in[q], 16 * (i // NB) + 16)
                else:
                    dve.wait_ge(r_in[q], (i - q) * (16 // NB) + 16)
                nc.vector.tensor_scalar(fx[p], rr[q][:, 0:D], rr[q][:, R_MEAN:R_MEAN + 1], rr[q][:, R_RSTD:R_RSTD + 1],
                                        ALU.subtract, ALU.mult).then_inc(f_xn, 1)

            def ft_copy(i, q):
                p = q % 2
                dve.wait_ge(f_tr, i + 1)
                nc.vector.tensor_copy(fxT[p], s2p[p][:, 0:P]).then_inc(f_xT, 1)

            def ft_out(i, q):
                p = q % 2
                dve.wait_ge(f_o, i + 1)
                if not isinstance(i, int) or i >= NB:
                    dve.wait_ge(scat[q], (i - q) * (16 // NB))
                nc.vector.scalar_tensor_tensor(out=fo[q], in0=(m0, m1)[p][:, 0:D], scalar=rr[q][:, R_GATE:R_GATE + 1],
                                               in1=rr[q][:, 0:D], op0=ALU.mult, op1=ALU.add).then_inc(f_out, 1)

            ft_norm(0, 0)

            for k in range(NB):
                ft_norm(k + 1, (k + 1) % NB)
                ft_copy(k, k)
                if k >= 2:
                    ft_out(k - 2, k - 2)
            with dve.Fori(1, NT // NB - 1, 1) as i:
                for q in range(NB):
                    ft_norm(NB * i + q + 1, (q + 1) % NB)
                    ft_copy(NB * i + q, q)
                    ft_out(NB * i + q - 2, (q + NB - 2) % NB)
            for k in range(NT - NB, NT + 2):
                if k + 1 < NT:
                    ft_norm(k + 1, (k + 1) % NB)
                if k < NT:
                    ft_copy(k, k % NB)
                ft_out(k - 2, (k - 2) % NB)

        @block.tensor
        def _(pe):
            pe.wait_ge(setup_p, 1)
            pe.wait_ge(w_in, 16 * NW)
            for g in range(2 * G):
                i = nc.tensor.matmul(m0[:, g:g + 1], brow[0:1, g // G, g % G].rearrange("p h r -> p (h r)"), one[0:1, 0:1],
                                     start=(g == 0), stop=True, skip_group_check=True)
            i.then_inc(setup_t, 1)
            nc.tensor.transpose(s1p[0][:, 0:NE * HH], b1s[:, :], ident[0:NE * HH, 0:NE * HH])
            nc.tensor.transpose(m1[0:GD, 0:P], wred[:, :], ident[:, :]).then_inc(setup_t, 1)
            pe.wait_ge(wgn_ok, 1)
            nc.tensor.transpose(m2[0:GD, 0:NE], wgn[:, :], ident[0:NE, 0:NE]).then_inc(setup_t, 1)
            pe.wait_ge(wgT_ok, 2)
            nc.tensor.matmul(pvp[:, 0:NE], wredT[:, :], wgT[:, :], start=True, stop=True).then_inc(setup_t, 1)
            pe.wait_ge(wc_ok, 1)
            pe.wait_ge(setup_a, 3)
            pe.wait_ge(setup_v, 3)

            def scores2(s, u, p):
                for g in range(G):
                    n = 2 * CU * (s - 2) + 2 * u + g
                    if u or not isinstance(s, int) or s >= 3:
                        pe.wait_ge(pt_ok, n - 1)
                    if u == 0:
                        pe.wait_ge(qd_a if g else qd_v, s - 1)
                    for b in range(2):
                        t = slice(UNIT * u + S * b, UNIT * u + S * b + S)
                        i = nc.tensor.matmul(s2p[g][S * b:S * b + S, :].rearrange("p (h q) -> p h q", h=GH),
                                             kT[p][:, g, t], Qd[p][:, g, :, t], start=True, stop=True)
                    i.then_inc(s2_ps, 1)

            def scores1(s, u, p):
                for g in range(G):
                    n = 2 * CU * (s - 1) + 2 * u + g
                    if u or not isinstance(s, int) or s >= 2:
                        pe.wait_ge(mx_ok, n - 1)
                    for b in range(2):
                        t = slice(UNIT * u + S * b, UNIT * u + S * b + S)
                        i = nc.tensor.matmul(s1p[g][S * b:S * b + S, :].rearrange("p (h q) -> p h q", h=GH),
                                             qb[:, g, t], Kd[p][:, g, :, t], start=True, stop=True)
                    i.then_inc(s1_ps, 1)

            def values(s, u, p):
                n = CU * (s - 2) + u
                pe.wait_ge(pt_ok, 2 * n + 2)
                if u == 0:
                    pe.wait_ge(v_sb, s - 1)
                    if not isinstance(s, int) or s >= 4:
                        pe.wait_ge(g_lgv, s - 3)
                if u or not isinstance(s, int) or s >= 3:
                    pe.wait_ge(ot_ok, n)
                for j in range(CJ):
                    nc.tensor.matmul(pvp[32 * j:32 * j + 32, CJ * S:2 * CJ * S], ksum[:, :],
                                     PT[u % 2][:, 4 * j:4 * j + 4, :].rearrange("p h q -> p (h q)"),
                                     start=True, stop=False, skip_group_check=True)
                for g in range(4):
                    for j in range(CJ):
                        i = nc.tensor.matmul(pvp[32 * j:32 * j + 32, S * g:S * g + S], V[p][:, u, 4 * j + g, :],
                                             PT[u % 2][:, 4 * j + g, :], start=False, stop=(g == 3), skip_group_check=True)
                i.then_inc(pv_ps, 1)

            def project_out(s, u):
                n = CU * (s - 2) + u
                pe.wait_ge(ot_ok, n + 1)
                if u or not isinstance(s, int) or s > 2:
                    pe.wait_ge(x1_ok, n)
                for g in range(4):
                    for b in range(2):
                        i = nc.tensor.matmul(m2[S * b:S * b + S, 0:D], OT[u % 2][:, g, :], wo[:, b, g, :],
                                             start=(g == 0), stop=(g == 3), skip_group_check=True)
                i.then_inc(o_ps, 1)

            def count(first, last, k):
                pe.wait_ge(oh_ok, k)
                o = oh[:, first:last, :].rearrange("p u e -> p (u e)")
                nc.tensor.matmul(pvp[:, 0:(last - first) * NE], tri[:, :], o, start=True, stop=True).then_inc(cnt_ps, 1)
                nc.tensor.matmul(m2[:, 0:(last - first) * NE], ones[:, :], o, start=True, stop=True).then_inc(cnt_ps, 1)

            def step(s, p, proj, peak, attend, gate):
                if proj:
                    pe.wait_ge(xn_ok, s + 1)
                    if not isinstance(s, int) or s >= 1:
                        pe.wait_ge(v_sb, s)
                    for u in range(CU):
                        i = nc.tensor.transpose(m0[:, UNIT * u:UNIT * u + UNIT], xn[:, u, :], ident[:, :])
                    i.then_inc(xT_ps, 1)
                    pe.wait_ge(c_in[p], 16 * (s // 2) + 16 if isinstance(s, int) else 8 * (s - p) + 16)
                    for u in range(CU):
                        i = nc.tensor.transpose(m1[:, UNIT * u:UNIT * u + UNIT], C[p][:, u, :], ident[:, :])
                    i.then_inc(cT_ps, 1)
                if peak:
                    pe.wait_ge(qb_ok, 2 * s)
                    pe.wait_ge(q_sb, 2 * s)
                    pe.wait_ge(kd_in[1 - p], kd_count(s, p))
                    scores1(s, 0, 1 - p)
                if attend:
                    scores2(s, 0, p)
                if peak:
                    scores1(s, 1, 1 - p)
                if proj:
                    pe.wait_ge(xT_sb, s + 1)
                    pe.wait_ge(cT_sb, s + 1)
                    for g, m in enumerate((m0, m1)):
                        nc.tensor.matmul(m[:, :], w16[:, 1, g].rearrange("p h r -> p (h r)"), cT[:, :], start=True,
                                         stop=True).then_inc(k_ps, 1)
                if attend:
                    if isinstance(s, int) and s == NC_ - 1:
                        pe.wait_ge(g_lgv, s - 3)
                        pe.wait_ge(x1_ok, CU * (s - 2))
                        count(0, UA, 1)
                        pe.wait_ge(cnt_rd, 1)
                    values(s, 0, p)
                if peak:
                    scores1(s, 2, 1 - p)
                if attend:
                    scores2(s, 1, p)
                    scores2(s, 2, p)
                    values(s, 1, p)
                    scores2(s, 3, p)
                    project_out(s, 0)
                if peak:
                    scores1(s, 3, 1 - p)
                if attend:
                    values(s, 2, p)
                if proj:
                    pe.wait_ge(k_sb, 2 * s + 2)
                    for u in range(CU):
                        i = nc.tensor.matmul(m0[:, D * u:D * u + D], cT[:, UNIT * u:UNIT * u + UNIT], wv[:, :],
                                             start=(u == 0), stop=(u == CU - 1), skip_group_check=True)
                    i.then_inc(v_ps, 1)
                if gate:
                    pe.wait_ge(g_cp, s - 2)
                    for u in range(CU):
                        i = nc.tensor.transpose(m1[:, UNIT * u:UNIT * u + UNIT], XC[p][:, u, :], ident[:, :])
                    i.then_inc(g_tr, 1)
                if attend:
                    project_out(s, 1)
                if peak:
                    pe.wait_ge(mx_ok, 2 * CU * s)
                    for g, m in enumerate(s1p):
                        for u in range(CU):
                            i = nc.tensor.transpose(m[:, UNIT * u:UNIT * u + UNIT],
                                                    mx[:, u, g].rearrange("p h r -> p (h r)"), ident[:, :])
                        i.then_inc(mT_ps, 1)
                if attend:
                    values(s, 3, p)
                if proj:
                    for g, m in enumerate(s1p):
                        if peak:
                            pe.wait_ge(qm_ok, 2 * (s - 1) + g + 1)
                        nc.tensor.matmul(m[:, :], w16[:, 0, g].rearrange("p h r -> p (h r)"), xT[:, :], start=True,
                                         stop=True).then_inc(q_ps, 1)
                if attend:
                    project_out(s, 2)
                if gate:
                    pe.wait_ge(g_xT, s - 2)
                    if attend:
                        pe.wait_ge(ot_ok, CU * (s - 1))
                    else:
                        pe.wait_ge(g_lgv, s - 3)
                    for u in range(CU):
                        i = nc.tensor.matmul(pvp[:, NE * u:NE * u + NE], cT[:, UNIT * u:UNIT * u + UNIT], wc[:, :],
                                             start=True, stop=True, skip_group_check=True)
                    i.then_inc(g_lg, 1)
                if attend:
                    project_out(s, 3)
            steps(pe, step)

            count(UA, NU, 2)

            pe.wait_ge(eid_ok, 1)
            pe.wait_ge(we_in, 16 * (2 + NE))
            def tstep(k, q, head, tail):
                p = q % 2
                if tail:
                    pe.wait_ge(f_xn, k + 1)
                    nc.tensor.transpose(s2p[p][:, 0:P], fx[p], ident[:, :]).then_inc(f_tr, 1)
                if head >= 1 and (tail or k == NT):
                    i, r = k - 1, 1 - p
                    pe.wait_ge(f_xT, i + 1)
                    pe.wait_ge(f_w, i + 1)
                    for m in range(HH):
                        j = nc.tensor.matmul(s1p[r][:, P * m:P * m + P], w1s[r][:, P * m:P * m + P], fxT[r],
                                             start=(m == 0), stop=(m == HH - 1), skip_group_check=True)
                    j.then_inc(f_h, 1)
                if head >= 2:
                    i = k - 2
                    e = pe.value_load(eid[0:1, bass.ds(i, 1)], min_val=0, max_val=NE - 1)
                    pe.wait_ge(f_g, i + 1)
                    if not isinstance(i, int) or i >= 2:
                        pe.wait_ge(f_out, i - 1)
                    for m in range(HH):
                        j = nc.tensor.matmul((m0, m1)[p][:, 0:D], fh[p][:, m, :],
                                             w2[:, bass.ds(e, 1), m, :].rearrange("p o c -> p (o c)"),
                                             start=(m == 0), stop=False)
                    nc.tensor.matmul((m0, m1)[p][:, 0:D], ones_row, b2r[:, bass.ds(e, 1), :].rearrange("p o c -> p (o c)"),
                                     start=False, stop=True).then_inc(f_o, 1)
            tiles(pe, tstep)


_INS = ["x", "ctx_1024", "g_xattn", "g_ffn", "L0_xattn_W_q", "L0_xattn_b_q", "L0_xattn_W_k", "L0_xattn_b_k",
        "L0_xattn_W_v", "L0_xattn_b_v", "L0_xattn_W_o", "L0_xattn_b_o", "L0_ffn_w_red", "L0_ffn_wg",
        "L0_ffn_W1", "L0_ffn_b1", "L0_ffn_W2", "L0_ffn_b2"]


def kernel(**inputs):
    import numpy as _np
    import concourse.bacc as _bacc
    from concourse import mybir as _mybir
    from concourse.bass_utils import run_bass_kernel_spmd as _run

    nc = _bacc.Bacc("TRN2", target_bir_lowering=False, num_devices=1)
    arrays, args = {}, []
    for name in _INS:
        a = _np.ascontiguousarray(inputs[name])
        arrays[f"in_{name}"] = a
        args.append(nc.dram_tensor(f"in_{name}", a.shape, _mybir.dt.from_np(a.dtype), kind="ExternalInput").ap())
    args.append(nc.dram_tensor("out_0", (B, S, D), F32, kind="ExternalOutput").ap())
    gated_block(nc, *args)
    r = _run(nc, [arrays], core_ids=[0])
    return r.results[0]["out_0"]
```
